# Optimizing a Trainium2 kernel written in Bass

```python
import numpy as np
import jax
import jax.numpy as jnp

def _softmax(x, axis=-1):
    return jax.nn.softmax(x, axis=axis)

def _gelu(x):
    return jax.nn.gelu(x, approximate=True)

def _silu(x):
    return jax.nn.silu(x)

def _sigmoid(x):
    return jax.nn.sigmoid(x)

def _layernorm(x, axis=-1, eps=1e-05):
    m = jnp.mean(x, axis=axis, keepdims=True)
    v = jnp.var(x, axis=axis, keepdims=True)
    return (x - m) / jnp.sqrt(v + eps)

def _scatter_add(tgt, idx, src, axis=0):
    return tgt.at[idx].add(src)

def _segment_sum(src, seg, n):
    return jax.ops.segment_sum(src, seg, n)
kernel_name = 'mk_adaln_attn_ffn_d1_seqx_r8_84e520'

def setup_inputs(seed: int=0):
    np.random.seed(seed)
    _w = jnp.asarray

    def _rec_inputs():
        import jax
        import jax.numpy as jnp
        _rk = jax.random.key(seed)
        x = -0.0003929 + 0.9999 * jax.random.normal(jax.random.fold_in(_rk, 1), (32, 32, 512), jnp.float32)
        _lenS = 32 - jax.random.randint(jax.random.fold_in(_rk, 7), (32,), 0, max(1, 32 // 4) + 1, jnp.int32)
        _lenS2 = 32 - jax.random.randint(jax.random.fold_in(_rk, 8), (32,), 0, max(1, 32 // 4) + 1, jnp.int32)
        itok_B_78_3631 = jax.random.randint(jax.random.fold_in(_rk, 11), (32,), 78, 454, jnp.int32)
        itok_Bx16_0_63 = jax.random.randint(jax.random.fold_in(_rk, 12), (32, 16), 0, 64, jnp.int32)
        itok_B_207_1644 = jax.random.randint(jax.random.fold_in(_rk, 13), (32,), 207, 1645, jnp.int32)
        return (x, itok_B_78_3631, itok_Bx16_0_63, itok_B_207_1644)
    x, itok_B_78_3631, itok_Bx16_0_63, itok_B_207_1644 = _rec_inputs()

    def _L0_cond_setup():
        import math
        import jax, jax.numpy as jnp
        import numpy as np
        B, H, N, L = (16, 32, 64, 512)
        DT_MIN, DT_MAX = (0.001, 0.1)

        def _get_kernel(log_dt, C, log_A_real, A_imag, length):
            dt = jnp.exp(log_dt)
            Cc = C[..., 0] + 1j * C[..., 1]
            A = -jnp.exp(log_A_real) + 1j * A_imag
            dtA = A * dt[:, None]
            Ct = Cc * (jnp.exp(dtA) - 1.0) / A
            P = dtA[:, :, None] * jnp.arange(length, dtype=jnp.float32)
            K = 2.0 * jnp.einsum('hn,hnl->hl', Ct, jnp.exp(P)).real
            return K
        key = jax.random.key(seed)
        ks = jax.random.split(key, 5)
        u = jax.random.normal(ks[0], (B, H, L), dtype=jnp.float32)
        log_dt = jax.random.uniform(ks[1], (H,), dtype=jnp.float32) * (math.log(DT_MAX) - math.log(DT_MIN)) + math.log(DT_MIN)
        C = jax.random.normal(ks[2], (H, N, 2), dtype=jnp.float32)
        log_A_real = jnp.log(0.5 * jnp.ones((H, N), dtype=jnp.float32))
        A_imag = math.pi * jnp.broadcast_to(jnp.arange(N, dtype=jnp.float32), (H, N))
        D = jax.random.normal(ks[3], (H,), dtype=jnp.float32)
        length = jax.random.randint(ks[4], (B,), 1, L + 1, dtype=jnp.int32)
        return {'u': u, 'log_dt': log_dt, 'C': C, 'log_A_real': log_A_real, 'A_imag': A_imag, 'D': D, 'length': length}
    _L0_cond_all = _L0_cond_setup()
    _L0_cond_in = {k: v for k, v in _L0_cond_all.items() if k in ('log_dt', 'C', 'log_A_real', 'A_imag', 'D')}
    del _L0_cond_all

    def _L0_attn_setup():
        import jax, jax.numpy as jnp
        import numpy as np
        B, S, EMB = (2, 256, 512)
        NHEADS, KVHEADS, HEAD_D = (32, 8, 128)
        SPLITS = (NHEADS * HEAD_D, KVHEADS * HEAD_D, KVHEADS * HEAD_D)
        key = jax.random.key(seed)
        k1, k2, k3 = jax.random.split(key, 3)
        q = jax.random.normal(k1, (B, S, EMB), dtype=jnp.float32)
        w_qkv = jax.random.normal(k2, (sum(SPLITS), EMB), dtype=jnp.float32) * 0.02
        w_dense = jax.random.normal(k3, (EMB, NHEADS * HEAD_D), dtype=jnp.float32) * 0.02
        return {'q': q, 'w_qkv': w_qkv, 'w_dense': w_dense}
    _L0_attn_all = _L0_attn_setup()
    _L0_attn_in = {k: v for k, v in _L0_attn_all.items() if k in ('w_qkv', 'w_dense')}
    del _L0_attn_all

    def _L0_cond2_setup():
        import jax, jax.numpy as jnp
        import numpy as np
        B, S, HID = (4, 128, 512)
        D, HQ, HK = (128, 32, 8)
        PAGES, PSIZE, NPP = (64, 32, 16)
        THETA = 10000.0
        EPS = 1e-06
        SCALE = 1.0 / float(np.sqrt(D))

        def _rmsnorm(t, w):
            var = jnp.mean(t * t, axis=-1, keepdims=True)
            return t * jax.lax.rsqrt(var + EPS) * w

        def _rope(t, pos):
            inv_freq = 1.0 / THETA ** (jnp.arange(0, D, 2, dtype=jnp.float32) / D)
            freqs = pos[..., None].astype(jnp.float32) * inv_freq
            cos = jnp.cos(freqs)[:, :, None, :]
            sin = jnp.sin(freqs)[:, :, None, :]
            t1, t2 = (t[..., :D // 2], t[..., D // 2:])
            return jnp.concatenate([t1 * cos - t2 * sin, t2 * cos + t1 * sin], axis=-1)
        key = jax.random.key(seed)
        ks = jax.random.split(key, 10)
        x = jax.random.normal(ks[0], (B, S, HID), jnp.float32)
        Wq = jax.random.normal(ks[1], (HQ * D, HID), jnp.float32) * 0.02
        Wk = jax.random.normal(ks[2], (HK * D, HID), jnp.float32) * 0.02
        Wv = jax.random.normal(ks[3], (HK * D, HID), jnp.float32) * 0.02
        Wo = jax.random.normal(ks[4], (HID, HQ * D), jnp.float32) * 0.02
        q_norm_w = jax.random.uniform(ks[5], (D,), jnp.float32)
        k_norm_w = jax.random.uniform(ks[6], (D,), jnp.float32)
        k_cache = jax.random.normal(ks[7], (PAGES, PSIZE, HK, D), jnp.float32)
        v_cache = jax.random.normal(ks[8], (PAGES, PSIZE, HK, D), jnp.float32)
        block_table = jnp.arange(B * NPP, dtype=jnp.int32).reshape(B, NPP)
        cache_seqlens = jax.random.randint(ks[9], (B,), 0, 475).astype(jnp.int32)
        return dict(x=x, Wq=Wq, Wk=Wk, Wv=Wv, Wo=Wo, q_norm_w=q_norm_w, k_norm_w=k_norm_w, k_cache=k_cache, v_cache=v_cache, block_table=block_table, cache_seqlens=cache_seqlens)
    _L0_cond2_all = _L0_cond2_setup()
    _L0_cond2_in = {k: v for k, v in _L0_cond2_all.items() if k in ('Wq', 'Wk', 'Wv', 'Wo', 'q_norm_w', 'k_norm_w', 'k_cache', 'v_cache')}
    del _L0_cond2_all

    def _L0_ffn_setup():
        import jax, jax.numpy as jnp
        import numpy as np
        B_, S, D_IN, D_OUT = (4, 256, 512, 512)
        N, RANK, ALPHA = (8, 16, 32)
        SCALE = ALPHA / RANK
        key = jax.random.key(seed)
        kx, ka, kb, kw, kbias = jax.random.split(key, 5)
        x = jax.random.normal(kx, (B_, S, D_IN), dtype=jnp.float32)
        lora_A = jax.random.normal(ka, (N, RANK, D_IN), dtype=jnp.float32) * (1.0 / np.sqrt(D_IN))
        lora_B = jax.random.normal(kb, (N, D_OUT, RANK), dtype=jnp.float32) * (1.0 / np.sqrt(RANK))
        W = jax.random.normal(kw, (D_OUT, D_IN), dtype=jnp.float32) * (1.0 / np.sqrt(D_IN))
        bias = jax.random.normal(kbias, (D_OUT,), dtype=jnp.float32) * 0.01
        lora_weights = jnp.full((N,), 1.0 / N, dtype=jnp.float32)
        return {'x': x, 'lora_A': lora_A, 'lora_B': lora_B, 'W': W, 'bias': bias, 'lora_weights': lora_weights}
    _L0_ffn_all = _L0_ffn_setup()
    _L0_ffn_in = {k: v for k, v in _L0_ffn_all.items() if k in ('lora_A', 'lora_B', 'W', 'bias', 'lora_weights')}
    del _L0_ffn_all
    return {'x': x, 'itok_B_78_3631': itok_B_78_3631, 'itok_Bx16_0_63': itok_Bx16_0_63, 'itok_B_207_1644': itok_B_207_1644, 'L0_cond_log_dt': _L0_cond_in['log_dt'], 'L0_cond_C': _L0_cond_in['C'], 'L0_cond_log_A_real': _L0_cond_in['log_A_real'], 'L0_cond_A_imag': _L0_cond_in['A_imag'], 'L0_cond_D': _L0_cond_in['D'], 'L0_attn_w_qkv': _L0_attn_in['w_qkv'], 'L0_attn_w_dense': _L0_attn_in['w_dense'], 'L0_cond2_Wq': _L0_cond2_in['Wq'], 'L0_cond2_Wk': _L0_cond2_in['Wk'], 'L0_cond2_Wv': _L0_cond2_in['Wv'], 'L0_cond2_Wo': _L0_cond2_in['Wo'], 'L0_cond2_q_norm_w': _L0_cond2_in['q_norm_w'], 'L0_cond2_k_norm_w': _L0_cond2_in['k_norm_w'], 'L0_cond2_k_cache': _L0_cond2_in['k_cache'], 'L0_cond2_v_cache': _L0_cond2_in['v_cache'], 'L0_ffn_lora_A': _L0_ffn_in['lora_A'], 'L0_ffn_lora_B': _L0_ffn_in['lora_B'], 'L0_ffn_W': _L0_ffn_in['W'], 'L0_ffn_bias': _L0_ffn_in['bias'], 'L0_ffn_lora_weights': _L0_ffn_in['lora_weights']}

def reference(x, itok_B_78_3631, itok_Bx16_0_63, itok_B_207_1644, L0_cond_log_dt, L0_cond_C, L0_cond_log_A_real, L0_cond_A_imag, L0_cond_D, L0_attn_w_qkv, L0_attn_w_dense, L0_cond2_Wq, L0_cond2_Wk, L0_cond2_Wv, L0_cond2_Wo, L0_cond2_q_norm_w, L0_cond2_k_norm_w, L0_cond2_k_cache, L0_cond2_v_cache, L0_ffn_lora_A, L0_ffn_lora_B, L0_ffn_W, L0_ffn_bias, L0_ffn_lora_weights):
    import jax
    import jax.numpy as jnp

    def _L0_cond_ref(u, log_dt, C, log_A_real, A_imag, D, length):
        import math
        import jax, jax.numpy as jnp
        import numpy as np
        B, H, N, L = (16, 32, 64, 512)
        DT_MIN, DT_MAX = (0.001, 0.1)

        def _get_kernel(log_dt, C, log_A_real, A_imag, length):
            dt = jnp.exp(log_dt)
            Cc = C[..., 0] + 1j * C[..., 1]
            A = -jnp.exp(log_A_real) + 1j * A_imag
            dtA = A * dt[:, None]
            Ct = Cc * (jnp.exp(dtA) - 1.0) / A
            P = dtA[:, :, None] * jnp.arange(length, dtype=jnp.float32)
            K = 2.0 * jnp.einsum('hn,hnl->hl', Ct, jnp.exp(P)).real
            return K
        Bq, Hq, Lq = u.shape
        K = _get_kernel(log_dt, C, log_A_real, A_imag, Lq)
        n = 2 * Lq
        kf = jnp.fft.rfft(K, n=n)
        uf = jnp.fft.rfft(u, n=n)
        y = jnp.fft.irfft(uf * kf[None], n=n)[..., :Lq]
        y = y + u * D[:, None]
        mask = (jnp.arange(Lq)[None, :] < length[:, None]).astype(u.dtype)
        return y * mask[:, None, :]

    def _L0_attn_ref(q, w_qkv, w_dense):
        import jax, jax.numpy as jnp
        import numpy as np
        B, S, EMB = (2, 256, 512)
        NHEADS, KVHEADS, HEAD_D = (32, 8, 128)
        SPLITS = (NHEADS * HEAD_D, KVHEADS * HEAD_D, KVHEADS * HEAD_D)
        Bq, Sq, _ = q.shape
        qkv = q @ w_qkv.T
        qs, ks, vs = jnp.split(qkv, np.cumsum(SPLITS)[:-1], axis=-1)
        G = NHEADS // KVHEADS
        qh = qs.reshape(Bq, Sq, KVHEADS, G, HEAD_D)
        kh = ks.reshape(Bq, Sq, KVHEADS, HEAD_D)
        vh = vs.reshape(Bq, Sq, KVHEADS, HEAD_D)
        scale = 1.0 / jnp.sqrt(jnp.float32(HEAD_D))
        scores = jnp.einsum('bskgd,btkd->bkgst', qh, kh) * scale
        causal = jnp.tril(jnp.ones((Sq, Sq), dtype=bool))
        scores = jnp.where(causal, scores, jnp.finfo(scores.dtype).min)
        probs = jax.nn.softmax(scores, axis=-1)
        attn = jnp.einsum('bkgst,btkd->bskgd', probs, vh)
        attn = attn.reshape(Bq, Sq, NHEADS * HEAD_D)
        return attn @ w_dense.T

    def _L0_cond2_ref(x, Wq, Wk, Wv, Wo, q_norm_w, k_norm_w, k_cache, v_cache, block_table, cache_seqlens):
        import jax, jax.numpy as jnp
        import numpy as np
        B, S, HID = (4, 128, 512)
        D, HQ, HK = (128, 32, 8)
        PAGES, PSIZE, NPP = (64, 32, 16)
        THETA = 10000.0
        EPS = 1e-06
        SCALE = 1.0 / float(np.sqrt(D))

        def _rmsnorm(t, w):
            var = jnp.mean(t * t, axis=-1, keepdims=True)
            return t * jax.lax.rsqrt(var + EPS) * w

        def _rope(t, pos):
            inv_freq = 1.0 / THETA ** (jnp.arange(0, D, 2, dtype=jnp.float32) / D)
            freqs = pos[..., None].astype(jnp.float32) * inv_freq
            cos = jnp.cos(freqs)[:, :, None, :]
            sin = jnp.sin(freqs)[:, :, None, :]
            t1, t2 = (t[..., :D // 2], t[..., D // 2:])
            return jnp.concatenate([t1 * cos - t2 * sin, t2 * cos + t1 * sin], axis=-1)
        bsz, seqlen, _ = x.shape
        q = jnp.einsum('bsd,ed->bse', x, Wq).reshape(bsz, seqlen, HQ, D)
        k = jnp.einsum('bsd,ed->bse', x, Wk).reshape(bsz, seqlen, HK, D)
        v = jnp.einsum('bsd,ed->bse', x, Wv).reshape(bsz, seqlen, HK, D)
        q = _rmsnorm(q, q_norm_w)
        k = _rmsnorm(k, k_norm_w)
        pos = cache_seqlens[:, None] + jnp.arange(seqlen)[None, :]
        q = _rope(q, pos)
        k = _rope(k, pos)
        L = NPP * PSIZE
        kc = k_cache[block_table].reshape(bsz, L, HK, D)
        vc = v_cache[block_table].reshape(bsz, L, HK, D)
        k_all = jnp.concatenate([kc, k], axis=1)
        v_all = jnp.concatenate([vc, v], axis=1)
        valid_c = jnp.arange(L)[None, :] < cache_seqlens[:, None]
        valid = jnp.concatenate([valid_c, jnp.ones((bsz, seqlen), dtype=bool)], axis=1)
        rep = HQ // HK
        k_all = jnp.repeat(k_all, rep, axis=2)
        v_all = jnp.repeat(v_all, rep, axis=2)
        scores = jnp.einsum('bqhd,bkhd->bhqk', q, k_all) * SCALE
        scores = jnp.where(valid[:, None, None, :], scores, -1e+30)
        probs = jax.nn.softmax(scores, axis=-1)
        o = jnp.einsum('bhqk,bkhd->bqhd', probs, v_all)
        o = o.reshape(bsz, seqlen, HQ * D)
        return jnp.einsum('bse,de->bsd', o, Wo)

    def _L0_ffn_ref(x, lora_A, lora_B, W, bias, lora_weights):
        import jax, jax.numpy as jnp
        import numpy as np
        B_, S, D_IN, D_OUT = (4, 256, 512, 512)
        N, RANK, ALPHA = (8, 16, 32)
        SCALE = ALPHA / RANK
        h = jnp.einsum('bsd,nrd->nbsr', x, lora_A)
        coef = (SCALE * lora_weights)[:, None, None]
        lora_out = jnp.einsum('nbsr,nor->bso', h, lora_B * coef)
        base = jnp.einsum('bsd,od->bso', x, W) + bias
        return base + lora_out
    x = x + _L0_attn_ref(_L0_cond_ref(x, L0_cond_log_dt, L0_cond_C, L0_cond_log_A_real, L0_cond_A_imag, L0_cond_D, itok_B_78_3631), L0_attn_w_qkv, L0_attn_w_dense)
    x = x + _L0_ffn_ref(_L0_cond2_ref(x, L0_cond2_Wq, L0_cond2_Wk, L0_cond2_Wv, L0_cond2_Wo, L0_cond2_q_norm_w, L0_cond2_k_norm_w, L0_cond2_k_cache, L0_cond2_v_cache, itok_Bx16_0_63, itok_B_207_1644), L0_ffn_lora_A, L0_ffn_lora_B, L0_ffn_W, L0_ffn_bias, L0_ffn_lora_weights)
    return x

_drawn_inputs = setup_inputs


def setup_inputs(seed=0):
    import zlib

    import numpy as np

    out = dict(_drawn_inputs(seed))
    spreads = {'L0_cond_log_A_real': (-0.6931471824645996, 0.6), 'L0_ffn_lora_weights': (0.125, 0.6)}
    factors = {'L0_cond2_Wk': 8.0,
     'L0_cond2_Wv': 5.659,
     'L0_cond2_k_norm_w': 8.0,
     'L0_ffn_bias': 5.96,
     'L0_cond2_k_cache': 3.343}
    for name, (base, spread) in spreads.items():
        noise = np.random.default_rng([zlib.crc32(name.encode()), seed]).standard_normal(out[name].shape)
        drawn = base * np.exp(spread * noise) if base else spread * noise
        out[name] = jnp.asarray(drawn.astype(out[name].dtype))
    for name, factor in factors.items():
        out[name] = (out[name] * factor).astype(out[name].dtype)
    return out
```

```python
from contextlib import ExitStack

import numpy as np

import concourse.bass as bass
from concourse import mybir

F32 = mybir.dt.float32
F32R = mybir.dt.float32r
I32 = mybir.dt.int32
ALU = mybir.AluOpType
ACT = mybir.ActivationFunctionType
X = mybir.AxisListType.X

P = 128
B, S, E = 32, 32, 512
TOK = B * S
EC = E // P
TT = TOK // P
HALF = TOK // 2
HQ, HK, D = 32, 8, 128
G = HQ // HK
N_MODES = 64
PAGES, PSIZE, NPP = 64, 32, 16
CACHE = NPP * PSIZE
KEYS = CACHE + S
SCALE = float(D) ** -0.5
THETA = 10000.0
EPS = 1e-6
LORA_N, RANK, LORA_SCALE = 8, 16, 2.0
BIG = 1e30
TWO_PI = 2.0 * np.pi
ROUND = 1.5 * 2.0 ** 23


def split_const(v, bits, n):
    parts = []
    for _ in range(n - 1):
        e = int(np.floor(np.log2(abs(v))))
        q = 2.0 ** (e - bits + 1)
        h = float(np.round(v / q) * q)
        parts.append(h)
        v -= h
    return parts + [float(v)]


PI2 = split_const(TWO_PI, 9, 4)
LN2 = split_const(float(np.log(2.0)), 12, 2)
EXP_TERMS = [1.0 / 5040, 1.0 / 720, 1.0 / 120, 1.0 / 24, 1.0 / 6, 0.5, 1.0]

I_STEPS, J_STEPS = 16, 32
ANG = 2 * I_STEPS + J_STEPS + 2
C_ID = 0
C_LSTEP = C_ID + P
C_SHIFT = C_LSTEP + ANG
C_RE = C_SHIFT + ANG
C_IM = C_RE + 1
C_LPOS = C_IM + 1
C_INVF = C_LPOS + EC
C_SPOS = C_INVF + D // 2
C_CAUSAL = C_SPOS + 1
C_KEYPOS = C_CAUSAL + S
C_PART = C_KEYPOS + KEYS
C_COLS = C_PART + 1


def constants():
    c = np.zeros((P, C_COLS), np.float32)
    p = np.arange(P)
    c[:, C_ID:C_ID + P] = np.eye(P)
    steps = np.concatenate([np.arange(I_STEPS) * J_STEPS, np.arange(I_STEPS) * J_STEPS, np.arange(J_STEPS), [1, 1]])
    c[:, C_LSTEP:C_LSTEP + ANG] = steps
    c[:, C_SHIFT:C_SHIFT + I_STEPS] = 0.25
    c[:64, C_SHIFT + 2 * I_STEPS:C_SHIFT + ANG - 2] = 0.25
    c[:, C_SHIFT + ANG - 2] = 0.25
    c[:64, C_RE] = 1
    c[64:, C_IM] = 1
    c[:, C_LPOS:C_LPOS + EC] = p[:, None] + P * np.arange(EC)
    c[:, C_INVF:C_INVF + D // 2] = np.float32(1.0) / np.float32(THETA) ** (np.arange(0, D, 2, dtype=np.float32) / np.float32(D))
    c[:, C_SPOS] = p % S
    c[:, C_CAUSAL:C_CAUSAL + S] = np.where(np.arange(S)[None, :] <= (p % S)[:, None], 0.0, -BIG)
    c[:, C_KEYPOS:C_KEYPOS + CACHE] = np.arange(CACHE)
    c[:, C_KEYPOS + CACHE:C_PART] = -BIG
    c[:, C_PART] = p
    return c


class Chain:

    def __init__(self, eng, sem):
        self.eng, self.sem, self.n = eng, sem, 0

    def __call__(self, instruction):
        self.n += 1
        instruction.then_inc(self.sem, 1)
        self.eng.wait_ge(self.sem, self.n)


def bc(ap, axis, shape):
    return ap.unsqueeze(axis).broadcast_to(shape)


def reduce_angle(step, v, ang, k, turns, row_shift):
    shape = list(ang.shape)
    step(v.tensor_scalar(k, ang, 1.0 / TWO_PI, None, ALU.mult))
    step(v.tensor_tensor(k, k, row_shift, ALU.add))
    step(v.tensor_scalar(k, k, ROUND, None, ALU.add))
    step(v.tensor_scalar(k, k, ROUND, None, ALU.subtract))
    for part in PI2:
        step(v.scalar_tensor_tensor(out=ang, in0=k, scalar=-part, in1=ang, op0=ALU.mult, op1=ALU.add))
    step(v.scalar_tensor_tensor(out=ang, in0=row_shift, scalar=TWO_PI, in1=ang, op0=ALU.mult, op1=ALU.add))
    step(v.tensor_scalar(ang, ang, float(np.float32(3.1415925)), float(np.float32(-3.1415925)), ALU.min, ALU.max))


def accurate_exp(step, v, x, r, k, ki):
    step(v.tensor_scalar(x, x, -87.0, 88.0, ALU.max, ALU.min))
    step(v.tensor_scalar(k, x, 1.0 / float(np.log(2.0)), ROUND, ALU.mult, ALU.add))
    step(v.tensor_scalar(k, k, ROUND, None, ALU.subtract))
    step(v.scalar_tensor_tensor(out=r, in0=k, scalar=-LN2[0], in1=x, op0=ALU.mult, op1=ALU.add))
    step(v.scalar_tensor_tensor(out=r, in0=k, scalar=-LN2[1], in1=r, op0=ALU.mult, op1=ALU.add))
    step(v.tensor_scalar(x, r, EXP_TERMS[0], None, ALU.mult))
    for term in EXP_TERMS[1:]:
        step(v.scalar_tensor_tensor(out=x, in0=x, scalar=term, in1=r, op0=ALU.add, op1=ALU.mult))
    step(v.tensor_scalar(ki, k, 127.0, None, ALU.add))
    step(v.tensor_scalar(ki, ki, 23, None, ALU.logical_shift_left))
    step(v.scalar_tensor_tensor(out=x, in0=x, scalar=1.0, in1=ki.bitcast(F32), op0=ALU.add, op1=ALU.mult))


def ssm_conv(nc, io, cst, x_res, y_hi, y_lo):
    with ExitStack() as ctx:
        sb = lambda name, shape, dt=F32: ctx.enter_context(nc.sbuf_tensor(name, shape, dt))
        ps = lambda name, shape: ctx.enter_context(nc.psum_tensor(name, shape, F32))
        sem = lambda name: ctx.enter_context(nc.semaphore(name))
        modes = sb("modes", [P, 5, B])
        expo = sb("expo", [P, 3, B])
        tmp = sb("tmp", [P, 10, B])
        tmpi = sb("tmpi", [P, 3, B], I32)
        ang = sb("ang", [P, B, ANG])
        turns = sb("turns", [P, B, ANG])
        mag = sb("mag", [P, B, ANG])
        coef = sb("coef", [P, B, I_STEPS])
        coef2 = sb("coef2", [P, B, I_STEPS])
        kern = sb("kern", [I_STEPS, B, J_STEPS])
        skip_row = sb("skip_row", [1, B])
        zeros = sb("zeros", [B, P])
        u_rev = sb("u_rev", [P, EC, S, B])
        toep = sb("toep", [P, 4, E])
        len_i = sb("len_i", [P, B], I32)
        len_f = sb("len_f", [P, B])
        keep = sb("keep", [P, EC, B])
        y = sb("y", [P, EC, B, S])
        p_kern = ps("p_kern", [I_STEPS, B * J_STEPS])
        p_conv = ps("p_conv", [P, 2, 4, EC, B])

        cst_in = sem("cst_in")
        par_in = sem("par_in")
        u_in = sem("u_in")
        dve_step = sem("dve_step_conv")
        act_step = sem("act_step_conv")
        angles_ready = sem("angles_ready")
        sines_ready = sem("sines_ready")
        coef_ready = sem("coef_ready")
        kern_done = sem("kern_done")
        kern_ready = sem("kern_ready")
        kern_out = sem("kern_out")
        toep_in = [sem(f"toep_in{i}") for i in range(4)]
        conv_done = sem("conv_done")
        y_ready = sem("y_ready")
        conv_taken = sem("conv_taken")
        split_done = sem("split_done")
        hi_ready = sem("hi_ready")
        kpad = io["kpad"]
        kp_rows = kpad.rearrange("(h m) -> h m", h=S)

        block = ctx.enter_context(nc.Block())

        @block.sync
        def _(sp):
            for i, name in enumerate(("log_dt_b", "log_A_real_t", "A_imag_t", "C_re_t", "C_im_t")):
                src = io[name]
                if i == 0:
                    sp.dma_start(modes[:, 0, :], src.partition_broadcast(P)).then_inc(par_in, 16)
                else:
                    for half in range(2):
                        sp.dma_start(modes[64 * half:64 * half + 64, i, :], src).then_inc(par_in, 16)
            sp.dma_start(skip_row[:, :], io["D"].rearrange("(o h) -> o h", o=1)).then_inc(par_in, 16)
            sp.dma_start(len_i[:, :], io["length"].partition_broadcast(P)).then_inc(par_in, 16)
            sp.dma_start(cst[:, :], io["cst"]).then_inc(cst_in, 16)
            sp.dma_start(u_rev[:, :, :, :].rearrange("p c s b -> p c (s b)"),
                         io["u_rev"].rearrange("(c p) n -> p c n", p=P)).then_inc(u_in, 16)
            sp.dma_start(x_res[:, :, :], io["xT"].rearrange("(c p) n -> p c n", p=P)).then_inc(u_in, 16)
            sp.wait_ge(kern_ready, 1)
            sp.dma_start(kp_rows[:, 0:P], zeros[:, :]).then_inc(kern_out, 16)
            sp.dma_start(kp_rows[:, P:P + E].rearrange("h (i j) -> i h j", i=I_STEPS), kern[:, :, :]).then_inc(kern_out, 16)
            sp.wait_ge(kern_out, 32)

            def load(s_at, slot):
                win = kpad[bass.ds(s_at * (P + E) + 1, P + E - 1)]
                win = bass.AP(tensor=win.tensor, offset=win.offset, ap=[[1, P], [1, E]])
                sp.dma_start(toep[:, slot, :], win).then_inc(toep_in[slot], 16)

            for s in range(S):
                if s >= 4:
                    sp.wait_ge(conv_done, s - 3)
                load(s, s % 4)
            sp.wait_ge(u_in, 32)

        @block.scalar
        def _(act):
            act.wait_ge(angles_ready, 1)
            nc.scalar.activation(mag[:, :, :], mag[:, :, :], ACT.Exp).then_inc(act_step, 1)
            nc.scalar.activation(ang[:, :, :], ang[:, :, :], ACT.Sin).then_inc(sines_ready, 1)
            for c in range(EC):
                act.wait_ge(y_ready, S // 4)
                nc.scalar.activation(y_hi[:, c, :], y[:, c, :, :].rearrange("p b s -> p (b s)"), ACT.Copy).then_inc(hi_ready, 1)

        @block.vector
        def _(v):
            step = Chain(v, dve_step)
            step(v.memset(zeros[:, :], 0.0))
            v.wait_ge(par_in, 16 * 11)
            v.wait_ge(cst_in, 16)
            step(v.tensor_copy(len_f[:, :], len_i[:, :]))
            for c in range(EC):
                step(v.tensor_scalar(keep[:, c, :], len_f[:, :], cst[:, C_LPOS + c:C_LPOS + c + 1], None, ALU.is_gt))
            step(v.tensor_copy(expo[:, 0:2, :], modes[:, 0:2, :]))
            accurate_exp(step, v, expo[:, 0:2, :], tmp[:, 0:2, :], tmp[:, 2:4, :], tmpi[:, 0:2, :])
            dt, ea, aim = expo[:, 0, :], expo[:, 1, :], modes[:, 2, :]
            d_re, d_im, a_re = tmp[:, 4, :], tmp[:, 5, :], tmp[:, 6, :]
            step(v.tensor_scalar(a_re, ea, -1.0, None, ALU.mult))
            step(v.tensor_tensor(d_re, a_re, dt, ALU.mult))
            step(v.tensor_tensor(d_im, aim, dt, ALU.mult))
            lstep = bc(cst[:, C_LSTEP:C_LSTEP + ANG], 1, [P, B, ANG])
            shift = bc(cst[:, C_SHIFT:C_SHIFT + ANG], 1, [P, B, ANG])
            step(v.tensor_tensor(ang[:, :, :], bc(d_im, 2, [P, B, ANG]), lstep, ALU.mult))
            step(v.tensor_tensor(mag[:, :, :], bc(d_re, 2, [P, B, ANG]), lstep, ALU.mult))
            reduce_angle(step, v, ang[:, :, :], turns[:, :, :], None, shift)
            v.tensor_copy(expo[:, 2, :], d_re).then_inc(angles_ready, 1)
            v.wait_ge(angles_ready, 1)
            accurate_exp(step, v, expo[:, 2, :], tmp[:, 0, :], tmp[:, 1, :], tmpi[:, 2, :])
            e_re, e_im, t0, t1 = tmp[:, 0, :], tmp[:, 1, :], tmp[:, 2, :], tmp[:, 3, :]
            c_re, c_im = modes[:, 3, :], modes[:, 4, :]
            v.wait_ge(sines_ready, 1)
            v.wait_ge(act_step, 1)
            step(v.tensor_tensor(e_re, expo[:, 2, :], ang[:, :, ANG - 2], ALU.mult))
            step(v.tensor_tensor(e_im, expo[:, 2, :], ang[:, :, ANG - 1], ALU.mult))
            step(v.tensor_scalar(e_re, e_re, -1.0, None, ALU.add))
            n_re, n_im = tmp[:, 7, :], tmp[:, 8, :]
            step(v.tensor_tensor(t0, c_re, e_re, ALU.mult))
            step(v.tensor_tensor(t1, c_im, e_im, ALU.mult))
            step(v.tensor_tensor(n_re, t0, t1, ALU.subtract))
            step(v.tensor_tensor(t0, c_re, e_im, ALU.mult))
            step(v.tensor_tensor(t1, c_im, e_re, ALU.mult))
            step(v.tensor_tensor(n_im, t0, t1, ALU.add))
            inv = tmp[:, 9, :]
            step(v.tensor_tensor(t0, a_re, a_re, ALU.mult))
            step(v.tensor_tensor(t1, aim, aim, ALU.mult))
            step(v.tensor_tensor(t0, t0, t1, ALU.add))
            step(v.reciprocal(inv, t0))
            ct_re, ct_im = e_re, e_im
            step(v.tensor_tensor(t0, n_re, a_re, ALU.mult))
            step(v.tensor_tensor(t1, n_im, aim, ALU.mult))
            step(v.tensor_tensor(ct_re, t0, t1, ALU.add))
            step(v.tensor_tensor(ct_re, ct_re, inv, ALU.mult))
            step(v.tensor_tensor(t0, n_im, a_re, ALU.mult))
            step(v.tensor_tensor(t1, n_re, aim, ALU.mult))
            step(v.tensor_tensor(ct_im, t0, t1, ALU.subtract))
            step(v.tensor_tensor(ct_im, ct_im, inv, ALU.mult))
            re_row, im_row = cst[:, C_RE:C_RE + 1], cst[:, C_IM:C_IM + 1]
            alpha, beta = n_re, n_im
            step(v.tensor_scalar(t0, ct_re, re_row, 2.0, ALU.mult, ALU.mult))
            step(v.tensor_scalar(t1, ct_im, im_row, -2.0, ALU.mult, ALU.mult))
            step(v.tensor_tensor(alpha, t0, t1, ALU.add))
            step(v.tensor_scalar(t0, ct_im, re_row, -2.0, ALU.mult, ALU.mult))
            step(v.tensor_scalar(t1, ct_re, im_row, -2.0, ALU.mult, ALU.mult))
            step(v.tensor_tensor(beta, t0, t1, ALU.add))
            step(v.tensor_tensor(ang[:, :, :], ang[:, :, :], mag[:, :, :], ALU.mult))
            step(v.tensor_tensor(coef[:, :, :], ang[:, :, 0:I_STEPS], bc(alpha, 2, [P, B, I_STEPS]), ALU.mult))
            step(v.tensor_tensor(coef2[:, :, :], ang[:, :, I_STEPS:2 * I_STEPS], bc(beta, 2, [P, B, I_STEPS]), ALU.mult))
            v.tensor_tensor(coef[:, :, :], coef[:, :, :], coef2[:, :, :], ALU.add).then_inc(coef_ready, 1)
            v.wait_ge(kern_done, 1)
            step(v.tensor_copy(kern[:, :, :].rearrange("i h j -> i (h j)"), p_kern[:, :]))
            v.tensor_tensor(kern[0:1, :, 0], kern[0:1, :, 0], skip_row[:, :], ALU.add).then_inc(kern_ready, 1)
            for q in range(S // 4):
                v.wait_ge(conv_done, 4 * q + 4)
                for c in range(EC):
                    last = v.tensor_tensor(y[:, c, :, 4 * q:4 * q + 4].rearrange("p b s -> p s b"),
                                           p_conv[:, q % 2, :, c, :],
                                           bc(keep[:, c, :], 1, [P, 4, B]), ALU.mult)
                last.then_inc(y_ready, 1)
            for c in range(EC):
                v.wait_ge(y_ready, S // 4)
                v.wait_ge(hi_ready, c + 1)
                v.tensor_tensor(y_lo[:, c, :], y[:, c, :, :].rearrange("p b s -> p (b s)"),
                                y_hi[:, c, :].bitcast(F32), ALU.subtract).then_inc(split_done, 1)

        @block.tensor
        def _(pe):
            pe.wait_ge(coef_ready, 1)
            for h in range(S):
                last = pe.matmul(p_kern[:, h * J_STEPS:(h + 1) * J_STEPS], coef[:, h, :],
                                 ang[:, h, 2 * I_STEPS:2 * I_STEPS + J_STEPS], start=True, stop=True)
            last.then_inc(kern_done, 1)
            pe.wait_ge(u_in, 32)
            for s in range(S):
                if s % 4 == 0 and s >= 8:
                    pe.wait_ge(y_ready, s // 4 - 1)
                pe.wait_ge(toep_in[s % 4], 16 * (s // 4 + 1))
                for d in range(EC):
                    last = pe.matmul(p_conv[:, s // 4 % 2, s % 4, d:EC, :], toep[:, s % 4, d * P:(d + 1) * P],
                                     u_rev[:, 0:EC - d, s, :], start=(d == 0 and s % 4 == 0), stop=(d == EC - 1),
                                     skip_group_check=True)
                last.then_inc(conv_done, 1)


def three_pass(pe, out, a_hi, a_lo, b_hi, b_lo, start, stop):
    pe.matmul(out, a_hi, b_hi, start=start, stop=False)
    pe.matmul(out, a_hi, b_lo, start=False, stop=False)
    return pe.matmul(out, a_lo, b_hi, start=False, stop=stop)


def gqa(nc, io, cst, x_res, y_hi, y_lo):
    with ExitStack() as ctx:
        sb = lambda name, shape, dt=F32: ctx.enter_context(nc.sbuf_tensor(name, shape, dt))
        sem = lambda name: ctx.enter_context(nc.semaphore(name))
        w_raw = sb("w_raw", [P, EC, 5 * D])
        w_hi = sb("w_hi", [P, EC, 5 * D], F32R)
        w_lo = sb("w_lo", [P, EC, 5 * D], F32R)
        wd_raw = sb("wd_raw", [P, G, E])
        wd_hi = sb("wd_hi", [P, G, E], F32R)
        wd_lo = sb("wd_lo", [P, G, E], F32R)
        q_t = sb("q_t", [P, B, G, S])
        k_t = sb("k_t", [P, TOK])
        o_hi = sb("o_hi", [P, G, TOK], F32R)
        o_lo = sb("o_lo", [P, G, TOK], F32R)
        v_nat = sb("v_nat", [P, TT, D])
        v_out = sb("v_out", [P, 2, E])
        probs = sb("probs", [P, 2, B // 2, S])
        probs_t = sb("probs_t", [P, 2, 4, P])
        top = sb("top", [P, 2, B // 2])
        total = sb("total", [P, 2, B // 2])
        p_proj = ctx.enter_context(nc.psum_tensor("p_proj", [P, 2, E], F32))
        p_score = ctx.enter_context(nc.psum_tensor("p_score", [P, 2, 4, P], F32))
        p_val = ctx.enter_context(nc.psum_tensor("p_val", [P, 4, 4, P], F32))
        ident = cst[:, C_ID:C_ID + P]
        causal = cst[:, C_CAUSAL:C_CAUSAL + S]

        w_in = sem("w_in")
        w_hi_ready = sem("w_hi_ready")
        w_lo_ready = sem("w_lo_ready")
        wd_in = sem("wd_in")
        wd_hi_ready = sem("wd_hi_ready")
        wd_lo_ready = sem("wd_lo_ready")
        proj_done = sem("proj_done")
        proj_taken = sem("proj_taken")
        v_stored = [sem(f"v_stored{i}") for i in range(2)]
        v_in = sem("v_in")
        scores_done = sem("scores_done")
        masked = sem("masked")
        top_ready = sem("top_ready")
        centred = sem("centred")
        exp_done = sem("exp_done")
        total_ready = sem("total_ready")
        inverse_ready = sem("inverse_ready")
        probs_ready = sem("probs_ready")
        turned = sem("turned")
        turned_taken = sem("turned_taken")
        val_done = sem("val_done")
        o_hi_ready = sem("o_hi_ready")
        o_lo_ready = sem("o_lo_ready")
        out_done = sem("out_done")
        out_added = sem("out_added")

        NV = 2
        VT = NV * TT
        QT = 2 * (G + 1)
        OT = 2 * EC
        w_qkv = io["w_qkv_t"].rearrange("(c p) n -> p c n", p=P)
        w_dense = io["w_dense_t"].rearrange("(m p) n -> p m n", p=P)
        v_rows = io["v_attn"].rearrange("(t p) n -> p t n", p=P)
        heads = lambda body, eng: (body(0, True, False), _loop(eng, 1, HK - 1, lambda k: body(k, False, False)),
                                   body(HK - 1, False, True))

        pick = lambda o, hf, j: o[:, :, :].rearrange("p g (hf bg j s) -> p hf j bg g s", hf=2, j=4, s=S)[:, hf, j]

        block = ctx.enter_context(nc.Block())

        @block.sync
        def _(sp):
            def load_w(n, first_col, cols, at):
                if not (isinstance(n, int) and n == 0):
                    sp.wait_ge(w_lo_ready, n)
                sp.dma_start(w_raw[:, :, at:at + cols], w_qkv[:, :, bass.ds(first_col, cols)]).then_inc(w_in, 16)

            for n in range(NV):
                load_w(n, (HQ + HK) * D + n * E, E, 0)
            for t in range(VT):
                if t == TT + 2:
                    load_w(NV, 0, E, 0)
                    sp.dma_start(w_raw[:, :, E:5 * D], w_qkv[:, :, HQ * D:HQ * D + D]).then_inc(w_in, 16)
                    sp.dma_start(wd_raw[:, :, :], w_dense[:, 0:G, :]).then_inc(wd_in, 16)
                sp.wait_ge(proj_taken, t + 1)
                sp.dma_start(v_rows[:, t % TT, t // TT * E:(t // TT + 1) * E], v_out[:, t % 2, :]).then_inc(v_stored[t % 2], 16)
            for i in range(2):
                sp.wait_ge(v_stored[i], 16 * VT // 2)

            def body(k, first, last):
                q_col, k_col, v_col = sp.snap(k * (G * D) + G * D), sp.snap(k * D + (HQ + 1) * D), sp.snap(k * D)
                d_row = sp.snap(k * G + G)
                if not first:
                    sp.wait_ge(val_done, 2 * k)
                sp.dma_start(v_nat[:, :, :], v_rows[:, :, bass.ds(v_col, D)]).then_inc(v_in, 16)
                if not last:
                    load_w(k + NV + 1, q_col, E, 0)
                    sp.dma_start(w_raw[:, :, E:5 * D], w_qkv[:, :, bass.ds(k_col, D)]).then_inc(w_in, 16)
                    sp.wait_ge(wd_lo_ready, k + 1)
                    sp.dma_start(wd_raw[:, :, :], w_dense[:, bass.ds(d_row, G), :]).then_inc(wd_in, 16)

            heads(body, sp)

        @block.scalar
        def _(act):
            def split_w(n, cols):
                act.wait_ge(w_in, (16 * (n + 1)) if isinstance(n, int) and n < NV else 32 * n - 16 * NV + 32)
                if not (isinstance(n, int) and n == 0):
                    act.wait_ge(proj_done, _w_used(n))
                nc.scalar.activation(w_hi[:, :, 0:cols], w_raw[:, :, 0:cols], ACT.Copy).then_inc(w_hi_ready, 1)

            def _w_used(n):
                return n * TT if isinstance(n, int) and n <= NV else (n - NV) * QT + VT

            split_w(0, E)
            for t in range(VT):
                if t == TT:
                    split_w(1, E)
                act.wait_ge(proj_done, t + 1)
                if t >= 2:
                    act.wait_ge(v_stored[t % 2], 16 * (t // 2))
                nc.scalar.activation(v_out[:, t % 2, :], p_proj[:, t % 2, :], ACT.Copy).then_inc(proj_taken, 1)
            split_w(NV, 5 * D)

            def copy_turned(k, hf):
                act.wait_ge(turned, 2 * k + hf + 1)
                nc.scalar.activation(probs_t[:, hf, :, :], p_score[:, hf, :, :], ACT.Copy).then_inc(turned_taken, 1)

            def exponentials(k, hf):
                act.wait_ge(centred, 2 * k + hf + 1)
                nc.scalar.activation(probs[:, hf, :, :], probs[:, hf, :, :], ACT.Exp).then_inc(exp_done, 1)

            def split_values(k, hf):
                act.wait_ge(val_done, 2 * k + hf + 1)
                for j in range(4):
                    nc.scalar.activation(pick(o_hi, hf, j), p_val[:, j, :, :].rearrange("p bg (g s) -> p bg g s", s=S),
                                         ACT.Copy).then_inc(o_hi_ready, 1)

            def body(k, first, last):
                for i in range(QT):
                    act.wait_ge(proj_done, k * QT + VT + i + 1)
                    hf, head = i // (G + 1), i % (G + 1)
                    if head < G:
                        to = q_t[:, hf * B // 2:(hf + 1) * B // 2, head, :]
                    else:
                        to = k_t[:, hf * HALF:(hf + 1) * HALF].rearrange("p (b s) -> p b s", s=S)
                    nc.scalar.activation(to, p_proj[:, i % 2, :].rearrange("p (b s) -> p b s", s=S), ACT.Copy).then_inc(proj_taken, 1)
                exponentials(k, 0)
                if not last:
                    split_w(k + NV + 1, 5 * D)
                copy_turned(k, 0)
                exponentials(k, 1)
                split_values(k, 0)
                copy_turned(k, 1)
                act.wait_ge(wd_in, 16 * k + 16)
                if not first:
                    act.wait_ge(out_done, k * OT)
                nc.scalar.activation(wd_hi[:, :, :], wd_raw[:, :, :], ACT.Copy).then_inc(wd_hi_ready, 1)
                split_values(k, 1)

            heads(body, act)

        @block.gpsimd
        def _(pool):
            for n in range(NV):
                pool.wait_ge(w_hi_ready, n + 1)
                nc.gpsimd.tensor_tensor(w_lo[:, :, 0:E], w_raw[:, :, 0:E], w_hi[:, :, 0:E].bitcast(F32), ALU.subtract).then_inc(w_lo_ready, 1)

            def split_lo(n):
                pool.wait_ge(w_hi_ready, n + 1)
                nc.gpsimd.tensor_tensor(w_lo[:, :, :], w_raw[:, :, :], w_hi[:, :, :].bitcast(F32), ALU.subtract).then_inc(w_lo_ready, 1)

            split_lo(NV)

            def body(k, first, last):
                if not last:
                    split_lo(k + NV + 1)
                pool.wait_ge(wd_hi_ready, k + 1)
                nc.gpsimd.tensor_tensor(wd_lo[:, :, :], wd_raw[:, :, :], wd_hi[:, :, :].bitcast(F32), ALU.subtract).then_inc(wd_lo_ready, 1)

            heads(body, pool)

        @block.vector
        def _(v):
            def centre(k, hf):
                n = 2 * k + hf + 1
                v.wait_ge(scores_done, n)
                v.scalar_tensor_tensor(out=probs[:, hf, :, :], in0=p_score[:, hf, :, :].rearrange("p a (b t) -> p (a b) t", t=S),
                                       scalar=SCALE, in1=bc(causal, 1, [P, B // 2, S]), op0=ALU.mult, op1=ALU.add).then_inc(masked, 1)
                v.wait_ge(masked, n)
                v.tensor_reduce(top[:, hf, :], probs[:, hf, :, :], X, ALU.max).then_inc(top_ready, 1)
                v.wait_ge(top_ready, n)
                v.tensor_tensor(probs[:, hf, :, :], probs[:, hf, :, :], bc(top[:, hf, :], 2, [P, B // 2, S]),
                                ALU.subtract).then_inc(centred, 1)

            def normalise(k, hf):
                n = 2 * k + hf + 1
                v.wait_ge(exp_done, n)
                v.tensor_reduce(total[:, hf, :], probs[:, hf, :, :], X, ALU.add).then_inc(total_ready, 1)
                v.wait_ge(total_ready, n)
                v.reciprocal(total[:, hf, :], total[:, hf, :]).then_inc(inverse_ready, 1)
                v.wait_ge(inverse_ready, n)
                v.tensor_tensor(probs[:, hf, :, :], probs[:, hf, :, :], bc(total[:, hf, :], 2, [P, B // 2, S]),
                                ALU.mult).then_inc(probs_ready, 1)

            def add_out(k, i):
                v.wait_ge(out_done, k * OT + i + 1)
                at = x_res[:, i % EC, i // EC * HALF:(i // EC + 1) * HALF]
                v.tensor_tensor(at, at, p_proj[:, i % 2, :], ALU.add).then_inc(out_added, 1)

            def split_values(k, hf):
                for j in range(4):
                    v.wait_ge(o_hi_ready, 8 * k + 4 * hf + j + 1)
                    v.tensor_tensor(pick(o_lo, hf, j), p_val[:, j, :, :].rearrange("p bg (g s) -> p bg g s", s=S),
                                    pick(o_hi, hf, j).bitcast(F32), ALU.subtract).then_inc(o_lo_ready, 1)

            def body(k, first, last):
                add = (lambda i: None) if first else (lambda i: add_out(k - 1, i))
                centre(k, 0)
                add(0)
                normalise(k, 0)
                add(1)
                add(2)
                centre(k, 1)
                add(3)
                split_values(k, 0)
                normalise(k, 1)
                for i in range(EC, OT):
                    add(i)
                split_values(k, 1)

            v.memset(top[:, :, :], 0.0).then_inc(out_added, 1)
            heads(body, v)
            for i in range(OT):
                add_out(HK - 1, i)

        @block.tensor
        def _(pe):
            for t in range(VT):
                if t % TT == 0:
                    pe.wait_ge(w_lo_ready, t // TT + 1)
                if t >= 2:
                    pe.wait_ge(proj_taken, t - 1)
                for c in range(EC):
                    at = slice(t % TT * P, (t % TT + 1) * P)
                    last_mm = three_pass(pe, p_proj[:, t % 2, :], y_hi[:, c, at], y_lo[:, c, at],
                                         w_hi[:, c, 0:E], w_lo[:, c, 0:E], c == 0, c == EC - 1)
                last_mm.then_inc(proj_done, 1)

            def product_tile(k, i, among, final=False):
                if i == 0:
                    pe.wait_ge(wd_lo_ready, k + 1)
                if i % EC == 0:
                    pe.wait_ge(o_lo_ready, 8 * k + 4 * (i // EC) + 4)
                if i < 2 and not final:
                    pe.wait_ge(proj_taken, (k + 1) * QT + VT + QT - 1 + i)
                else:
                    pe.wait_ge(out_added, k * OT + i)
                to = slice(i % EC * P, (i % EC + 1) * P)
                at = slice(i // EC * HALF, (i // EC + 1) * HALF)
                for g in range(G):
                    last_mm = three_pass(pe, p_proj[:, i % 2, :], wd_hi[:, g, to], wd_lo[:, g, to],
                                         o_hi[:, g, at], o_lo[:, g, at], g == 0, g == G - 1)
                    if g == G - 1:
                        last_mm.then_inc(out_done, 1)
                    among(g)

            def score(k, hf, n, first):
                if n == 0 and not first:
                    pe.wait_ge(turned_taken, 2 * k + hf - 1)
                b = hf * B // 2 + n
                mm = pe.matmul(p_score[:, hf, n // 4, n % 4 * S:(n % 4 + 1) * S], q_t[:, b, :, :].rearrange("p g s -> p (g s)"),
                               k_t[:, b * S:(b + 1) * S], start=True, stop=True)
                if n == B // 2 - 1:
                    mm.then_inc(scores_done, 1)

            def transposes(k, hf):
                pe.wait_ge(probs_ready, 2 * k + hf + 1)
                for bg in range(4):
                    mm = pe.transpose(p_score[:, hf, bg, :], probs[:, hf, 4 * bg:4 * bg + 4, :].rearrange("p b t -> p (b t)"), ident)
                mm.then_inc(turned, 1)

            def values(k, hf, first):
                if hf == 0:
                    pe.wait_ge(v_in, 16 * k + 16)
                pe.wait_ge(turned_taken, 2 * k + hf + 1)
                if not (first and hf == 0):
                    pe.wait_ge(o_lo_ready, 8 * k + 4 * hf)
                for n in range(B // 2):
                    bg, j = n // 4, n % 4
                    rows = slice(S * j, S * j + S)
                    mm = pe.matmul(p_val[:, j, bg, :], v_nat[rows, hf * 4 + bg, :], probs_t[rows, hf, bg, :],
                                   start=True, stop=True)
                mm.then_inc(val_done, 1)

            def body(k, first, last):
                pe.wait_ge(w_lo_ready, k + NV + 1)
                if not first:
                    pe.wait_ge(out_added, k * OT - OT + 1)
                for i in range(QT):
                    hf, head = i // (G + 1), i % (G + 1)
                    pe.wait_ge(proj_taken, k * QT + VT + i - 1)
                    at = slice(hf * HALF, (hf + 1) * HALF)
                    m = slice(head * D, (head + 1) * D)
                    for c in range(EC):
                        last_mm = three_pass(pe, p_proj[:, i % 2, :], w_hi[:, c, m], w_lo[:, c, m],
                                             y_hi[:, c, at], y_lo[:, c, at], c == 0, c == EC - 1)
                        if c == EC - 1:
                            last_mm.then_inc(proj_done, 1)
                        if i > G + 1:
                            score(k, 0, (i - G - 2) * EC + c, first)
                if first:
                    pe.wait_ge(proj_taken, k * QT + VT + QT)
                    for n in range(B // 2):
                        score(k, 1, n, first)
                    for hf in range(2):
                        transposes(k, hf)
                        values(k, hf, first)
                    return
                for i in range(OT):
                    hf = i // EC

                    def among(g):
                        if 0 < i < EC:
                            n = (i - 1) * (G + 1) + g + min(g, 1)
                            for n in ((n, n + 1) if g == 0 else (n,)):
                                score(k, 1, n, first)
                            if i == EC - 1 and g == G - 1:
                                score(k, 1, B // 2 - 1, first)

                    if i % EC == EC - 1:
                        transposes(k, hf)
                    product_tile(k - 1, i, among)
                    if i % EC == EC - 1:
                        values(k, hf, first)

            heads(body, pe)
            for i in range(OT):
                product_tile(HK - 1, i, lambda g: None, final=True)


def _loop(eng, start, end, body):
    with eng.Fori(start, end) as i:
        body(i)


QKV_CHUNKS = (HQ + 2 * HK) * D // E
LAG = 3


def cached_qkv(nc, io, cst, x_res):
    with ExitStack() as ctx:
        sb = lambda name, shape, dt=F32: ctx.enter_context(nc.sbuf_tensor(name, shape, dt))
        sem = lambda name: ctx.enter_context(nc.semaphore(name))
        x_hi = sb("x_hi", [P, EC, TOK], F32R)
        x_lo = sb("x_lo", [P, EC, TOK], F32R)
        w_raw = sb("w3_raw", [P, 2, EC, E])
        w_hi = sb("w3_hi", [P, 2, EC, E], F32R)
        w_lo = sb("w3_lo", [P, 2, EC, E], F32R)
        len_i = sb("len3_i", [P, TT], I32)
        pos = sb("pos", [P, TT])
        quarter = sb("quarter", [P, 2])
        ang = sb("ang3", [P, 2, TT, D // 2])
        turns = sb("turns3", [P, 2, TT, D // 2])
        norm_w = sb("norm_w", [P, 2, D])
        rot = sb("rot", [P, 2, 2, TT, D])
        squares = sb("squares", [P, 4, 4])
        rms = sb("rms", [P, 4, 4])
        eps = sb("eps", [P, 1])
        inv_rms = sb("inv_rms", [P, 4, 4])
        normed = sb("normed", [P, 4, 4, D])
        part_a = sb("part_a", [P, 4, 4, D])
        part_b = sb("part_b", [P, 4, 4, D])
        stage = sb("stage", [P, 4, 4, 4, S])
        v_out = sb("v3_out", [P, 2, E])
        p_tile = ctx.enter_context(nc.psum_tensor("p_tile", [P, 4, E], F32))
        p_turn = ctx.enter_context(nc.psum_tensor("p_turn", [P, 2, 4, P], F32))
        ident = cst[:, C_ID:C_ID + P]

        len_in = sem("len_in")
        w_in = [sem(f"w3_in{i}") for i in range(2)]
        step_s = sem("rot_step")
        angles3 = sem("angles3")
        sines3 = sem("sines3")
        x_hi_ready = sem("x_hi_ready")
        x_lo_ready = sem("x_lo_ready")
        hi_piece = sem("hi_piece")
        lo_piece = sem("lo_piece")
        tile_done = sem("tile_done")
        tile_taken = sem("tile_taken")
        v_stored = [sem(f"v3_stored{i}") for i in range(2)]
        squares_ready = sem("squares_ready")
        rms_ready = sem("rms_ready")
        inv_ready = sem("inv_ready")
        a_ready = sem("a_ready")
        b_ready = sem("b_ready")
        rotated = sem("rotated")
        half_rotated = sem("half_rotated")
        turned = sem("turned3")
        staged = sem("staged")
        stored = [sem(f"stored{i}") for i in range(4)]

        w_all = io["w_vkq_t"].rearrange("(c p) n -> p c n", p=P)
        v_rows = io["v_new"].rearrange("(t p) n -> p t n", p=P)
        qk = io["qk_new"]
        PAIR = 2 * TT
        PAIRS = QKV_CHUNKS // 2
        pairs = lambda body, eng: (body(1, True, False), _loop(eng, 2, PAIRS - 1, lambda m: body(m, False, False)),
                                   body(PAIRS - 1, False, True))

        block = ctx.enter_context(nc.Block())

        @block.sync
        def _(sp):
            for bq in range(4):
                src = io["cache_len"].rearrange("(t q) -> q t", q=4)[bq]
                sp.dma_start(len_i[S * bq:S * bq + S, :], src.partition_broadcast(S), allow_slow_non_contiguous=True).then_inc(len_in, 16)
            sp.dma_start(norm_w[:, 0, :], io["q_norm"].partition_broadcast(P)).then_inc(len_in, 16)
            sp.dma_start(norm_w[:, 1, :], io["k_norm"].partition_broadcast(P)).then_inc(len_in, 16)

            def load_w(n, slot, col):
                if not (isinstance(n, int) and n < 2):
                    sp.wait_ge(lo_piece, (n - 1) * EC)
                sp.dma_start(w_raw[:, slot, :, :], w_all[:, :, bass.ds(col, E)]).then_inc(w_in[slot], 16)

            load_w(0, 0, 0)
            load_w(1, 1, E)
            for t in range(PAIR):
                if t % TT == 4:
                    load_w(t // TT + 2, t // TT, (t // TT + 2) * E)
                sp.wait_ge(tile_taken, t + 1)
                sp.dma_start(v_rows[:, t % TT, t // TT * E:(t // TT + 1) * E], v_out[:, t % 2, :]).then_inc(v_stored[t % 2], 16)

            def body(m, first, last):
                cols = [sp.snap((2 * m + 2 + i) * E) for i in range(2)]
                to = [sp.snap((2 * m - 2 + i) * P) for i in range(2)]
                for i in range(PAIR):
                    if i % TT == 4 and not last:
                        load_w(2 * m + 2 + i // TT, i // TT, cols[i // TT])
                    sp.wait_ge(staged, (m - 1) * PAIR + i + 1)
                    b0 = i % TT * 4
                    sp.dma_start(qk[b0:b0 + 4, :, bass.ds(to[i // TT], P)].rearrange("b d n -> d b n"),
                                 stage[:, i % 4, :, :, :].rearrange("d b h s -> d b (h s)")).then_inc(stored[i % 4], 16)

            pairs(body, sp)
            for i in range(4):
                sp.wait_ge(stored[i], 16 * (PAIRS - 1) * PAIR // 4)
            for i in range(2):
                sp.wait_ge(v_stored[i], 16 * PAIR // 2)

        @block.scalar
        def _(act):
            for c in range(EC):
                nc.scalar.activation(x_hi[:, c, :], x_res[:, c, :], ACT.Copy).then_inc(x_hi_ready, 1)
            act.wait_ge(angles3, 1)
            nc.scalar.activation(ang[:, :, :, :], ang[:, :, :, :], ACT.Sin).then_inc(sines3, 1)
            for t in range(PAIR):
                act.wait_ge(tile_done, t + 1)
                if t >= 2:
                    act.wait_ge(v_stored[t % 2], 16 * (t // 2))
                nc.scalar.activation(v_out[:, t % 2, :], p_tile[:, t % 4, :], ACT.Copy).then_inc(tile_taken, 1)

            def normalise(m, i):
                u = (m - 1) * PAIR + i
                act.wait_ge(inv_ready, u + 1)
                for h in range(4):
                    ins = nc.scalar.activation(normed[:, i % 4, h, :], p_tile[:, i % 4, h * D:(h + 1) * D], ACT.Copy,
                                               scale=inv_rms[:, i % 4, h:h + 1])
                ins.then_inc(tile_taken, 1)

            def body(m, first, last):
                for i in range(PAIR):
                    act.wait_ge(tile_done, m * PAIR + i + 1)
                    if not (first and i < 4):
                        act.wait_ge(rotated, (m - 1) * PAIR + i - 3)
                    for h in range(4):
                        ins = nc.scalar.activation(normed[:, i % 4, h, :], p_tile[:, i % 4, h * D:(h + 1) * D], ACT.Square,
                                                   accum_out=squares[:, i % 4, h:h + 1])
                    ins.then_inc(squares_ready, 1)
                    act.wait_ge(squares_ready, (m - 1) * PAIR + i + 1)
                    nc.scalar.activation(rms[:, i % 4, :], squares[:, i % 4, :], ACT.Sqrt, bias=eps[:, :], scale=1.0 / D).then_inc(rms_ready, 1)
                    if i >= 1:
                        normalise(m, i - 1)
                    elif not first:
                        normalise(m - 1, PAIR - 1)

            pairs(body, act)
            normalise(PAIRS - 1, PAIR - 1)

        @block.gpsimd
        def _(pool):
            def split_lo(n, slot, c):
                pool.wait_ge(hi_piece, n * EC + c + 1)
                nc.gpsimd.tensor_tensor(w_lo[:, slot, c, :], w_raw[:, slot, c, :], w_hi[:, slot, c, :].bitcast(F32),
                                        ALU.subtract).then_inc(lo_piece, 1)

            for n in range(3):
                for c in range(EC):
                    split_lo(n, n % 2, c)

            def with_sine(m, i, key):
                u = (m - 1) * PAIR + i
                pool.wait_ge(tile_taken, m * PAIR + i + 1)
                if not (isinstance(u, int) and u < 4):
                    pool.wait_ge(rotated, u - 3)
                nc.gpsimd.tensor_tensor(part_b[:, i % 4, :, :], normed[:, i % 4, :, :],
                                        bc(rot[:, key, 1, i % TT, :], 1, [P, 4, D]), ALU.mult).then_inc(b_ready, 1)

            def tiles(m, key, carried, last=False):
                for i in range(PAIR):
                    if i >= 1:
                        with_sine(m, i - 1, key)
                    elif carried:
                        with_sine(m - 1, PAIR - 1, 0)
                    if i % TT < EC and not (last and i >= TT):
                        split_lo(2 * m + 1 + i // TT, (1 + i // TT) % 2, i % TT)

            tiles(1, 1, False)
            with_sine(1, PAIR - 1, 1)
            tiles(2, 0, False)
            _loop(pool, 3, PAIRS - 1, lambda m: tiles(m, 0, True))
            tiles(PAIRS - 1, 0, True, True)
            with_sine(PAIRS - 1, PAIR - 1, 0)

        @block.vector
        def _(v):
            step = Chain(v, step_s)
            def split_hi(n, slot, c):
                if c == 0:
                    v.wait_ge(w_in[slot], 8 * (n - slot) + 16)
                    if not (isinstance(n, int) and n < 2):
                        v.wait_ge(tile_done, (n - 1) * TT)
                v.tensor_copy(w_hi[:, slot, c, :], w_raw[:, slot, c, :]).then_inc(hi_piece, 1)

            for c in range(EC):
                v.wait_ge(x_hi_ready, c + 1)
                v.tensor_tensor(x_lo[:, c, :], x_res[:, c, :], x_hi[:, c, :].bitcast(F32), ALU.subtract).then_inc(x_lo_ready, 1)
            for n in range(2):
                for c in range(EC):
                    split_hi(n, n, c)
            v.wait_ge(len_in, 16 * 6)
            step(v.tensor_copy(pos[:, :], len_i[:, :]))
            step(v.tensor_scalar(pos[:, :], pos[:, :], cst[:, C_SPOS:C_SPOS + 1], None, ALU.add))
            step(v.memset(eps[:, :], EPS))
            step(v.memset(quarter[:, 0:1], 0.25))
            step(v.memset(quarter[:, 1:2], 0.0))
            for f in range(2):
                step(v.tensor_tensor(ang[:, f, :, :], bc(pos[:, :], 2, [P, TT, D // 2]),
                                     bc(cst[:, C_INVF:C_INVF + D // 2], 1, [P, TT, D // 2]), ALU.mult))
            flat = lambda a: a[:, :, :, :].rearrange("p f t d -> p f (t d)")
            reduce_angle(step, v, flat(ang), flat(turns), None, bc(quarter[:, :], 2, [P, 2, TT * D // 2]))
            v.engine_nop().then_inc(angles3, 1)
            step(v.tensor_scalar(norm_w[:, 0, :], norm_w[:, 0, :], -SCALE, None, ALU.mult))
            v.wait_ge(sines3, 1)
            for which in range(2):
                for f in range(2):
                    for hf in range(2):
                        at = slice(hf * D // 2, (hf + 1) * D // 2)
                        w = bc(norm_w[:, which, at], 1, [P, TT, D // 2])
                        step(v.tensor_tensor(rot[:, which, f, :, at], ang[:, f, :, :], w, ALU.mult))
                step(v.tensor_scalar(rot[:, which, 1, :, D // 2:D], rot[:, which, 1, :, D // 2:D], -1.0, None, ALU.mult))

            def invert(m, i):
                u = (m - 1) * PAIR + i
                v.wait_ge(rms_ready, u + 1)
                v.reciprocal(inv_rms[:, i % 4, :], rms[:, i % 4, :]).then_inc(inv_ready, 1)

            def rotate(m, i, key):
                u = (m - 1) * PAIR + i
                v.wait_ge(tile_taken, m * PAIR + i + 1)
                if not (isinstance(u, int) and u < 4):
                    v.wait_ge(turned, u - 3)
                v.tensor_tensor(part_a[:, i % 4, :, :], normed[:, i % 4, :, :],
                                bc(rot[:, key, 0, i % TT, :], 1, [P, 4, D]), ALU.mult).then_inc(a_ready, 1)
                v.wait_ge(a_ready, u + 1)
                v.wait_ge(b_ready, u + 1)
                lo, hi = slice(0, D // 2), slice(D // 2, D)
                v.tensor_tensor(part_a[:, i % 4, :, lo], part_a[:, i % 4, :, lo], part_b[:, i % 4, :, hi], ALU.add).then_inc(half_rotated, 1)
                v.tensor_tensor(part_a[:, i % 4, :, hi], part_a[:, i % 4, :, hi], part_b[:, i % 4, :, lo], ALU.add).then_inc(rotated, 1)

            def put(m, i):
                u = (m - 1) * PAIR + i
                v.wait_ge(turned, u + 1)
                if not (isinstance(u, int) and u < 4):
                    v.wait_ge(stored[i % 4], 4 * (u - i % 4))
                v.tensor_copy(stage[:, i % 4, :, :, :].rearrange("p b h s -> p h b s"),
                              p_turn[:, i % 2, :, :].rearrange("p h (b s) -> p h b s", s=S)).then_inc(staged, 1)

            def at(m, i, first, act_on, *more):
                if i >= 0:
                    act_on(m, i, *more)
                elif not first:
                    act_on(m - 1, PAIR + i, *more)

            def tiles(m, key, rotates_before, puts_before, last=False):
                for i in range(PAIR):
                    at(m, i - 4, not puts_before, put)
                    if i % TT < EC and not (last and i >= TT):
                        split_hi(2 * m + 1 + i // TT, (1 + i // TT) % 2, i % TT)
                    invert(m, i)
                    at(m, i - 2, not rotates_before, rotate, key)

            for c in range(EC):
                split_hi(2, 0, c)
            tiles(1, 1, False, False)
            for i in range(PAIR - 2, PAIR):
                rotate(1, i, 1)
            tiles(2, 0, False, True)
            _loop(v, 3, PAIRS - 1, lambda m: tiles(m, 0, True, True))
            tiles(PAIRS - 1, 0, True, True, True)
            for i in range(PAIR, PAIR + 4):
                put(PAIRS - 1, i - 4)
                if i < PAIR + 2:
                    rotate(PAIRS - 1, i - 2, 0)

        @block.tensor
        def _(pe):
            def project(m, i):
                t = m * PAIR + i
                if i % TT == 0:
                    pe.wait_ge(lo_piece, (2 * m + i // TT + 1) * EC)
                if not (isinstance(t, int) and t < 4):
                    pe.wait_ge(tile_taken, t - 3)
                rows = slice(i % TT * P, (i % TT + 1) * P)
                for c in range(EC):
                    mm = three_pass(pe, p_tile[:, i % 4, :], x_hi[:, c, rows], x_lo[:, c, rows],
                                    w_hi[:, i // TT, c, :], w_lo[:, i // TT, c, :], c == 0, c == EC - 1)
                mm.then_inc(tile_done, 1)

            def turn(m, i):
                u = (m - 1) * PAIR + i
                pe.wait_ge(rotated, u + 1)
                if not (isinstance(u, int) and u < 2):
                    pe.wait_ge(staged, u - 1)
                for h in range(4):
                    mm = pe.transpose(p_turn[:, i % 2, h, :], part_a[:, i % 4, h, :], ident)
                mm.then_inc(turned, 1)

            pe.wait_ge(x_lo_ready, EC)
            for i in range(PAIR):
                project(0, i)

            def body(m, first, last):
                for i in range(PAIR):
                    project(m, i)
                    if i >= LAG:
                        turn(m, i - LAG)
                    elif not first:
                        turn(m - 1, PAIR + i - LAG)

            body(1, True, False)
            _loop(pe, 2, PAIRS, lambda m: body(m, False, False))
            for i in range(PAIR - LAG, PAIR):
                turn(PAIRS - 1, i)


def cached_attention(nc, io, cst):
    with ExitStack() as ctx:
        sb = lambda name, shape, dt=F32: ctx.enter_context(nc.sbuf_tensor(name, shape, dt))
        sem = lambda name: ctx.enter_context(nc.semaphore(name))
        KW = HK * S
        keys = sb("keys", [P, 2, NPP + 1, HK, S])
        vals = sb("vals", [P, 2, NPP // 4 + 1, HK * D])
        queries = sb("queries", [P, 2, HQ * S])
        outs = sb("outs", [P, 2, HQ * S])
        pages = sb("pages", [P, B * NPP], I32)
        pages_f = sb("pages_f", [P, B * NPP])
        rows = sb("rows", [P, B, NPP // 4 + NPP], I32)
        rows_now = sb("rows_now", [P, 2, NPP // 4 + NPP], I32)
        len_i = sb("len4_i", [P, B], I32)
        len_f = sb("len4_f", [P, B])
        mask = sb("mask", [P, 2, KEYS])
        probs = sb("probs4", [P, 2, KEYS])
        low = sb("low", [P, 2])
        wait_carrier = sb("wait_carrier", [P, 1])
        pool_carrier = sb("pool_carrier", [P, 4])
        total = sb("total4", [P, 2])
        inverse = sb("inverse4", [P, 2])
        probs_t = sb("probs4_t", [P, 2, 5, P])
        p_score = ctx.enter_context(nc.psum_tensor("p4_score", [P, 2, 2 * E], F32))
        p_turn = ctx.enter_context(nc.psum_tensor("p4_turn", [P, 2, 4, P], F32))
        p_val = ctx.enter_context(nc.psum_tensor("p4_val", [P, 2, E], F32))
        ident = cst[:, C_ID:C_ID + P]

        table_in = sem("table_in")
        kq_in = [sem(f"kq_in{i}") for i in range(2)]
        v_new_in = [sem(f"v_new_in{i}") for i in range(2)]
        keys_gathered = [sem(f"keys_gathered{i}") for i in range(2)]
        vals_gathered = [sem(f"vals_gathered{i}") for i in range(2)]
        len_ready = sem("len_ready")
        pages_ready = sem("pages_ready")
        rows_ready = sem("rows_ready")
        rows_placed = sem("rows_placed")
        mask_ready = sem("mask_ready")
        scores_done = sem("scores4_done")
        masked = sem("masked4")
        exp_done = sem("exp4_done")
        inverse_ready = sem("inverse4_ready")
        probs_ready = sem("probs4_ready")
        turned = sem("turned4")
        main_taken = sem("main_taken")
        new_taken = sem("new_taken")
        val_done = sem("val4_done")
        out_ready = sem("out4_ready")
        out_stored = [sem(f"out_stored{i}") for i in range(2)]

        SP_PAGES = range(0, NPP, 2)
        LOADS = 16 * (len(SP_PAGES) + 2)
        GATHERS = 16 * (NPP - len(SP_PAGES))
        VALS = 16 * (NPP // 4)
        RB = 2 * HK
        k_pages, v_pages = io["k_pages"], io["v_pages"]
        qk, v_new, o_dram = io["qk_new"], io["v_new"], io["o_new"]
        both = lambda body, eng: (body(0, True), _loop(eng, 1, B // 2, lambda m: body(m, False)))

        block = ctx.enter_context(nc.Block())

        @block.sync
        def _(sp):
            sp.dma_start(pages[:, :], io["block_table"].partition_broadcast(P)).then_inc(table_in, 16)
            sp.dma_start(len_i[:, :], io["cache_len"].partition_broadcast(P)).then_inc(table_in, 16)
            sp.wait_ge(table_in, 32)

            def store(m, slot):
                sp.wait_ge(out_ready, m * RB + (slot + 1) * HK)
                b = sp.snap(2 * m + slot) if not isinstance(m, int) else 2 * m + slot
                sp.dma_start(o_dram[bass.ds(b, 1), :, :].rearrange("o d n -> (o d) n"), outs[:, slot, :]).then_inc(out_stored[slot], 16)

            def body(m, first):
                for slot in range(2):
                    b = 2 * m + slot
                    done = kq_in[slot]
                    if not first:
                        sp.wait_ge(scores_done, (b - 1) * HK)
                    mine = qk[bass.ds(b, 1), :, :].rearrange("o d n -> (o d) n")
                    sp.dma_start(queries[:, slot, :], mine[:, KW:KW + HQ * S]).then_inc(done, 16)
                    sp.dma_start(keys[:, slot, NPP, :, :].rearrange("p h s -> p (h s)"), mine[:, 0:KW]).then_inc(done, 16)
                    for j in SP_PAGES:
                        page = sp.value_load(pages[0:1, bass.ds(b * NPP + j, 1)], min_val=0, max_val=PAGES - 1)
                        sp.dma_start(keys[:, slot, j, :, :].rearrange("p h s -> p (h s)"),
                                     k_pages[bass.ds(page, 1), :, :].rearrange("o d n -> (o d) n")).then_inc(done, 16)
                    row = sp.snap(b * S)
                    if not first:
                        store(m - 1, slot)
                    sp.dma_start(vals[0:S, slot, NPP // 4, :], v_new[bass.ds(row, S), :]).then_inc(v_new_in[slot], 16)

            both(body, sp)
            for slot in range(2):
                store(B // 2 - 1, slot)
            for slot in range(2):
                sp.wait_ge(out_stored[slot], 16 * B // 2)

        @block.gpsimd
        def _(pool):
            k_flat = k_pages.rearrange("o d n -> (o d) n")
            v_flat = v_pages.rearrange("o t n -> (o t) n")

            def gather(to, rows, source, done):
                pool.indirect_dma_start(to, None, source, bass.IndirectOffsetOnAxis(ap=rows, axis=0)).then_inc(done, 16)

            def hold_wait(n):
                one = pool_carrier[:, 2:3]
                nc.gpsimd.tensor_tensor(pool_carrier[:, n:n + 1], one, one, ALU.mult)

            pool.wait_ge(rows_ready, 5)
            pool.wait_ge(len_ready, 1)

            def body(m, first):
                for slot in range(2):
                    b = 2 * m + slot
                    if not first:
                        pool.wait_ge(scores_done, (b - 1) * HK)
                    row = pool.snap(b) if not first else b
                    if not first:
                        hold_wait(0)
                    nc.gpsimd.tensor_copy(rows_now[:, slot, :], rows[:, bass.ds(row, 1), :].rearrange("p o n -> p (o n)")).then_inc(rows_placed, 1)
                    pool.wait_ge(rows_placed, b + 1)
                    hold_wait(1)
                    for j in range(NPP):
                        if j not in SP_PAGES:
                            gather(keys[:, slot, j, :, :].rearrange("p h s -> p (h s)"),
                                   rows_now[:, slot, NPP // 4 + j:NPP // 4 + j + 1], k_flat, keys_gathered[slot])
                    if not first:
                        pool.wait_ge(val_done, (b - 1) * HK)
                        hold_wait(3)
                    for n in range(NPP // 4):
                        gather(vals[:, slot, n, :], rows_now[:, slot, n:n + 1], v_flat, vals_gathered[slot])

            both(body, pool)

        def step_of(m, i, first, what):
            if i >= 0:
                what(m, i)
            elif not first:
                what(m - 1, RB + i)

        @block.scalar
        def _(act):
            def exponent(m, i):
                r = m * RB + i
                act.wait_ge(masked, r + 1)
                nc.scalar.activation(probs[:, i % 2, :], probs[:, i % 2, :], ACT.Exp, bias=low[:, i % 2:i % 2 + 1],
                                     scale=-1.0, accum_out=total[:, i % 2:i % 2 + 1]).then_inc(exp_done, 1)

            def take_turned(m, i):
                r = m * RB + i
                act.wait_ge(turned, r + 1)
                if not (isinstance(r, int) and r < 2):
                    act.wait_ge(val_done, r - 1)
                nc.scalar.activation(probs_t[:, i % 2, 0:4, :], p_turn[:, 0, :, :], ACT.Copy).then_inc(main_taken, 1)

            def take_values(m, i):
                r = m * RB + i
                slot, k = i // HK, i % HK
                act.wait_ge(val_done, r + 1)
                if k == 0 and not (isinstance(m, int) and m == 0):
                    act.wait_ge(out_stored[slot], 16 * m)
                nc.scalar.activation(outs[:, slot, k * P:(k + 1) * P], p_val[:, i % 2, 0:P], ACT.Copy).then_inc(out_ready, 1)

            def body(m, first):
                for i in range(RB):
                    exponent(m, i)
                    step_of(m, i - 1, first, take_turned)
                    step_of(m, i - 2, first, take_values)

            both(body, act)
            take_turned(B // 2 - 1, RB - 1)
            take_values(B // 2 - 1, RB - 2)
            take_values(B // 2 - 1, RB - 1)

        @block.vector
        def _(v):
            v.memset(pool_carrier[:, :], 1.0).then_inc(len_ready, 1)
            v.wait_ge(table_in, 32)
            v.tensor_copy(len_f[:, :], len_i[:, :]).then_inc(len_ready, 1)
            v.tensor_copy(pages_f[:, :], pages[:, :]).then_inc(pages_ready, 1)
            v.wait_ge(pages_ready, 1)
            v.tensor_scalar(rows[:, :, NPP // 4:], pages_f[:, :].rearrange("p (b j) -> p b j", b=B), float(D), cst[:, C_PART:C_PART + 1], ALU.mult, ALU.add).then_inc(rows_ready, 1)
            for q in range(4):
                at = slice(S * q, S * q + S)
                v.tensor_scalar(rows[at, :, 0:NPP // 4], pages_f[at, :].rearrange("p (b n q) -> p q b n", b=B, q=4)[:, q], float(PSIZE),
                                cst[at, C_SPOS:C_SPOS + 1], ALU.mult, ALU.add).then_inc(rows_ready, 1)
            v.wait_ge(len_ready, 2)

            def make_mask(m, slot):
                b = 2 * m + slot
                v.tensor_scalar(mask[:, slot, :], cst[:, C_KEYPOS:C_KEYPOS + KEYS], len_f[:, bass.ds(b, 1)], BIG,
                                ALU.is_ge, ALU.mult).then_inc(mask_ready, 1)

            def mask_scores(m, i):
                r = m * RB + i
                v.wait_ge(scores_done, r + 1)
                if not (isinstance(r, int) and r < 2):
                    v.wait_ge(turned, r - 1)
                v.memset(wait_carrier[:, :], 0.0)
                v.tensor_tensor_reduce(out=probs[:, i % 2, :], in0=p_score[:, i % 2, 0:KEYS], in1=mask[:, i // HK, :],
                                       scale=1.0, scalar=3e38, op0=ALU.add, op1=ALU.min,
                                       accum_out=low[:, i % 2:i % 2 + 1]).then_inc(masked, 1)

            def normalise(m, i):
                r = m * RB + i
                v.wait_ge(exp_done, r + 1)
                v.reciprocal(inverse[:, i % 2:i % 2 + 1], total[:, i % 2:i % 2 + 1]).then_inc(inverse_ready, 1)
                v.wait_ge(inverse_ready, r + 1)
                v.tensor_scalar(probs[:, i % 2, :], probs[:, i % 2, :], inverse[:, i % 2:i % 2 + 1], None,
                                ALU.mult).then_inc(probs_ready, 1)

            def take_new(m, i):
                r = m * RB + i
                v.wait_ge(turned, r + 1)
                if not (isinstance(r, int) and r < 2):
                    v.wait_ge(val_done, r - 1)
                v.tensor_copy(probs_t[0:S, i % 2, 4, :], p_turn[0:S, 1, 0, :]).then_inc(new_taken, 1)

            def body(m, first):
                for i in range(RB):
                    if i % HK == 0:
                        make_mask(m, i // HK)
                        v.wait_ge(mask_ready, 2 * m + i // HK + 1)
                    mask_scores(m, i)
                    step_of(m, i - 1, first, take_new)
                    normalise(m, i)

            both(body, v)
            take_new(B // 2 - 1, RB - 1)

        @block.tensor
        def _(pe):
            def scores(m, i):
                r = m * RB + i
                slot, k = i // HK, i % HK
                if k == 0:
                    pe.wait_ge(kq_in[slot], LOADS * m + LOADS)
                    pe.wait_ge(keys_gathered[slot], GATHERS * m + GATHERS)
                if not (isinstance(r, int) and r < 2):
                    pe.wait_ge(masked, r - 1)
                q = queries[:, slot, k * P:(k + 1) * P]
                pe.matmul(p_score[:, i % 2, 0:CACHE], q, keys[:, slot, 0:NPP, k, :], start=True, stop=True)
                pe.matmul(p_score[:, i % 2, CACHE:KEYS], q, keys[:, slot, NPP, k, :], start=True, stop=True).then_inc(scores_done, 1)

            def transposes(m, i):
                r = m * RB + i
                pe.wait_ge(probs_ready, r + 1)
                if not (isinstance(r, int) and r < 1):
                    pe.wait_ge(main_taken, r)
                    pe.wait_ge(new_taken, r)
                for n in range(4):
                    pe.transpose(p_turn[:, 0, n, :], probs[:, i % 2, n * P:(n + 1) * P], ident)
                pe.transpose(p_turn[0:S, 1, 0, :], probs[:, i % 2, CACHE:KEYS], ident).then_inc(turned, 1)

            def values(m, i):
                r = m * RB + i
                slot, k = i // HK, i % HK
                if k == 0:
                    pe.wait_ge(vals_gathered[slot], VALS * m + VALS)
                    pe.wait_ge(v_new_in[slot], 16 * m + 16)
                pe.wait_ge(main_taken, r + 1)
                pe.wait_ge(new_taken, r + 1)
                if not (isinstance(r, int) and r < 2):
                    pe.wait_ge(out_ready, r - 1)
                cols = slice(k * D, (k + 1) * D)
                for n in range(4):
                    pe.matmul(p_val[:, i % 2, 0:P], vals[:, slot, n, cols], probs_t[:, i % 2, n, :], start=(n == 0), stop=False)
                pe.matmul(p_val[:, i % 2, 0:P], vals[0:S, slot, 4, cols], probs_t[0:S, i % 2, 4, :], start=False,
                          stop=True).then_inc(val_done, 1)

            def body(m, first):
                for i in range(RB):
                    scores(m, i)
                    step_of(m, i - 1, first, transposes)
                    step_of(m, i - 2, first, values)

            both(body, pe)
            transposes(B // 2 - 1, RB - 1)
            values(B // 2 - 1, RB - 2)
            values(B // 2 - 1, RB - 1)


def output_ffn(nc, io, cst, x_res):
    with ExitStack() as ctx:
        sb = lambda name, shape, dt=F32: ctx.enter_context(nc.sbuf_tensor(name, shape, dt))
        sem = lambda name: ctx.enter_context(nc.semaphore(name))
        o_raw = sb("o_raw", [P, 2, B, G * S])
        o_hi = sb("o5_hi", [P, 2, B, G * S], F32R)
        o_lo = sb("o5_lo", [P, B, G * S], F32R)
        w_raw = sb("w5_raw", [P, 2, G, E])
        w_hi = sb("w5_hi", [P, 2, G, E], F32R)
        w_lo = sb("w5_lo", [P, 2, G, E], F32R)
        y3 = sb("y3", [P, EC, TOK])
        lora_a = sb("lora_a", [P, E])
        lora_b = sb("lora_b", [P, E])
        lora_c = sb("lora_c", [P, 1])
        w_ffn = sb("w_ffn", [P, EC, E])
        bias = sb("bias", [P, EC])
        p_out = ctx.enter_context(nc.psum_tensor("p_out", [P, 4, E], F32))
        p_lora = ctx.enter_context(nc.psum_tensor("p_lora", [P, 4, E], F32))

        ow_in = [sem(f"ow_in{i}") for i in range(2)]
        ffn_in = sem("ffn_in")
        o_hi_ready = sem("o5_hi_ready")
        o_lo_ready = sem("o5_lo_ready")
        w_hi_ready = sem("w5_hi_ready")
        w_lo_ready = sem("w5_lo_ready")
        out_done = sem("out5_done")
        out_added = sem("out5_added")
        lora_step = sem("lora_step")
        lora_done = sem("lora_done")
        ffn_ready = sem("ffn_ready")
        ffn_done = sem("ffn_done")
        final_ready = sem("final_ready")
        final_out = sem("final_out")
        OT = 2 * EC
        w_o = io["w_o_t"].rearrange("(m p) n -> p m n", p=P)
        o_all = io["o_new"].rearrange("b d n -> d b n")
        both = lambda body, eng: (body(0, True), _loop(eng, 1, HK // 2, lambda m: body(m, False)))

        block = ctx.enter_context(nc.Block())

        @block.sync
        def _(sp):
            def body(m, first):
                for slot in range(2):
                    k = 2 * m + slot
                    oc, wr = sp.snap(k * P), sp.snap(k * G)
                    if not first:
                        sp.wait_ge(o_lo_ready, k - 1)
                        sp.wait_ge(w_lo_ready, k - 1)
                    sp.dma_start(o_raw[:, slot, :, :], o_all[:, :, bass.ds(oc, P)]).then_inc(ow_in[slot], 16)
                    sp.dma_start(w_raw[:, slot, :, :], w_o[:, bass.ds(wr, G), :]).then_inc(ow_in[slot], 16)
                if first:
                    for to, name in ((lora_a[:, :], "lora_a"), (lora_b[:, :], "lora_b_t")):
                        sp.dma_start(to, io[name]).then_inc(ffn_in, 16)
                    lw = io["lora_w"]
                    sp.dma_start(lora_c[:, :], bc(lw, 1, [LORA_N, RANK]).unsqueeze(2), allow_slow_non_contiguous=True).then_inc(ffn_in, 16)
                    sp.dma_start(w_ffn[:, :, :], io["w_ffn_t"].rearrange("(c p) n -> p c n", p=P)).then_inc(ffn_in, 16)
                    sp.dma_start(bias[:, :], io["bias"].rearrange("(c p) -> p c", p=P), allow_slow_non_contiguous=True).then_inc(ffn_in, 16)

            both(body, sp)
            rows = io["out_t"].rearrange("(c p) n -> p c n", p=P)
            for i in range(OT):
                at = slice(i % 2 * HALF, (i % 2 + 1) * HALF)
                sp.wait_ge(final_ready, i + 1)
                sp.dma_start(rows[:, i // 2, at], x_res[:, i // 2, at]).then_inc(final_out, 16)
            sp.wait_ge(final_out, 16 * OT)

        @block.scalar
        def _(act):
            def body(m, first):
                for slot in range(2):
                    k = 2 * m + slot
                    act.wait_ge(ow_in[slot], 32 * m + 32)
                    if not first:
                        act.wait_ge(out_done, OT * (k - 1))
                    nc.scalar.activation(w_hi[:, slot, :, :], w_raw[:, slot, :, :], ACT.Copy).then_inc(w_hi_ready, 1)
                    nc.scalar.activation(o_hi[:, slot, :, :], o_raw[:, slot, :, :], ACT.Copy).then_inc(o_hi_ready, 1)

            both(body, act)

        @block.gpsimd
        def _(pool):
            def body(m, first):
                for slot in range(2):
                    k = 2 * m + slot
                    pool.wait_ge(w_hi_ready, k + 1)
                    nc.gpsimd.tensor_tensor(w_lo[:, slot, :, :], w_raw[:, slot, :, :], w_hi[:, slot, :, :].bitcast(F32),
                                            ALU.subtract).then_inc(w_lo_ready, 1)

            both(body, pool)

        @block.vector
        def _(v):
            def split_o(k, slot):
                v.wait_ge(o_hi_ready, k + 1)
                v.tensor_tensor(o_lo[:, :, :], o_raw[:, slot, :, :], o_hi[:, slot, :, :].bitcast(F32),
                                ALU.subtract).then_inc(o_lo_ready, 1)

            def body(m, first):
                for slot in range(2):
                    k = 2 * m + slot
                    if not (first and slot == 0):
                        v.wait_ge(out_done, OT * k)
                    split_o(k, slot)
                    for i in range(OT):
                        v.wait_ge(out_done, OT * k + i + 1)
                        at = y3[:, i // 2, i % 2 * HALF:(i % 2 + 1) * HALF]
                        if first and slot == 0:
                            v.tensor_copy(at, p_out[:, i % 4, :]).then_inc(out_added, 1)
                        else:
                            v.tensor_tensor(at, at, p_out[:, i % 4, :], ALU.add).then_inc(out_added, 1)

            v.wait_ge(ffn_in, 16 * 5)
            v.tensor_scalar(lora_c[:, :], lora_c[:, :], LORA_SCALE, None, ALU.mult).then_inc(lora_step, 1)
            v.wait_ge(lora_step, 1)
            v.tensor_scalar(lora_b[:, :], lora_b[:, :], lora_c[:, 0:1], None, ALU.mult).then_inc(lora_step, 1)
            both(body, v)
            v.wait_ge(lora_done, 1)
            v.tensor_tensor(w_ffn[:, :, :], w_ffn[:, :, :], p_lora[:, :, :], ALU.add).then_inc(ffn_ready, 1)
            for i in range(OT):
                v.wait_ge(ffn_done, i + 1)
                at = x_res[:, i // 2, i % 2 * HALF:(i % 2 + 1) * HALF]
                v.scalar_tensor_tensor(out=at, in0=p_out[:, i % 4, :], scalar=bias[:, i // 2:i // 2 + 1], in1=at,
                                       op0=ALU.add, op1=ALU.add).then_inc(final_ready, 1)

        @block.tensor
        def _(pe):
            pe.wait_ge(lora_step, 2)
            for c in range(EC):
                mm = pe.matmul(p_lora[:, c, :], lora_a[:, c * P:(c + 1) * P], lora_b[:, :], start=True, stop=True)
            mm.then_inc(lora_done, 1)

            def body(m, first):
                for slot in range(2):
                    k = 2 * m + slot
                    pe.wait_ge(w_lo_ready, k + 1)
                    pe.wait_ge(o_lo_ready, k + 1)
                    for i in range(OT):
                        if not (first and slot == 0 and i < 4):
                            pe.wait_ge(out_added, k * OT + i - 3)
                        to = slice(i // 2 * P, (i // 2 + 1) * P)
                        bs = slice(i % 2 * B // 2, (i % 2 + 1) * B // 2)
                        for g in range(G):
                            gs = slice(g * S, (g + 1) * S)
                            mm = three_pass(pe, p_out[:, i % 4, :], w_hi[:, slot, g, to], w_lo[:, slot, g, to],
                                            o_hi[:, slot, bs, gs], o_lo[:, bs, gs], g == 0, g == G - 1)
                        mm.then_inc(out_done, 1)

            both(body, pe)
            pe.wait_ge(ffn_ready, 1)
            for i in range(OT):
                pe.wait_ge(out_added, HK * OT)
                if i >= 4:
                    pe.wait_ge(final_ready, i - 3)
                for c in range(EC):
                    mm = pe.matmul(p_out[:, i % 4, :], w_ffn[:, c, i // 2 * P:(i // 2 + 1) * P],
                                   y3[:, c, i % 2 * HALF:(i % 2 + 1) * HALF], start=(c == 0), stop=(c == EC - 1))
                mm.then_inc(ffn_done, 1)


def layouts(inputs):
    def lay(a):
        return np.ascontiguousarray(a)

    x = np.asarray(inputs["x"])
    u = x.transpose(2, 1, 0).reshape(EC, P, S * B)[:, ::-1]
    wqkv = np.asarray(inputs["L0_attn_w_qkv"]).T
    c = np.asarray(inputs["L0_cond_C"])
    return {
        "xT": lay(x.reshape(TOK, E).T),
        "u_rev": lay(u.reshape(E, S * B)),
        "length": lay(inputs["itok_B_78_3631"]),
        "log_dt_b": lay(inputs["L0_cond_log_dt"]),
        "log_A_real_t": lay(np.asarray(inputs["L0_cond_log_A_real"]).T),
        "A_imag_t": lay(np.asarray(inputs["L0_cond_A_imag"]).T),
        "C_re_t": lay(c[..., 0].T),
        "C_im_t": lay(c[..., 1].T),
        "D": lay(inputs["L0_cond_D"]),
        "w_qkv_t": lay(wqkv),
        "w_dense_t": lay(np.asarray(inputs["L0_attn_w_dense"]).T),
        "w_vkq_t": lay(np.concatenate([inputs["L0_cond2_Wv"], inputs["L0_cond2_Wk"], inputs["L0_cond2_Wq"]]).T),
        "cache_len": lay(inputs["itok_B_207_1644"]),
        "block_table": lay(np.asarray(inputs["itok_Bx16_0_63"]).reshape(B * NPP)),
        "q_norm": lay(inputs["L0_cond2_q_norm_w"]),
        "k_norm": lay(inputs["L0_cond2_k_norm_w"]),
        "k_pages": lay(np.asarray(inputs["L0_cond2_k_cache"]).transpose(0, 3, 2, 1).reshape(PAGES, D, HK * PSIZE)),
        "v_pages": lay(np.asarray(inputs["L0_cond2_v_cache"]).reshape(PAGES, PSIZE, HK * D)),
        "w_o_t": lay(np.asarray(inputs["L0_cond2_Wo"]).T),
        "lora_a": lay(np.asarray(inputs["L0_ffn_lora_A"]).reshape(LORA_N * RANK, E)),
        "lora_b_t": lay(np.asarray(inputs["L0_ffn_lora_B"]).transpose(0, 2, 1).reshape(LORA_N * RANK, E)),
        "lora_w": lay(inputs["L0_ffn_lora_weights"]),
        "w_ffn_t": lay(np.asarray(inputs["L0_ffn_W"]).T),
        "bias": lay(inputs["L0_ffn_bias"]),
        "cst": constants(),
    }


def build(nc, io):
    io["kpad"] = nc.dram_tensor("kpad", (S * (P + E),), F32, kind="Internal").ap()
    io["v_attn"] = nc.dram_tensor("v_attn", (TOK, HK * D), F32, kind="Internal").ap()
    io["v_new"] = nc.dram_tensor("v_new", (TOK, HK * D), F32, kind="Internal").ap()
    io["qk_new"] = nc.dram_tensor("qk_new", (B, D, (HK + HQ) * S), F32, kind="Internal").ap()
    io["o_new"] = nc.dram_tensor("o_new", (B, D, HQ * S), F32, kind="Internal").ap()
    with ExitStack() as ctx:
        cst = ctx.enter_context(nc.sbuf_tensor("cst", [P, C_COLS], F32))
        x_res = ctx.enter_context(nc.sbuf_tensor("x_res", [P, EC, TOK], F32))
        with ExitStack() as ctx2:
            y_hi = ctx2.enter_context(nc.sbuf_tensor("y_hi", [P, EC, TOK], F32R))
            y_lo = ctx2.enter_context(nc.sbuf_tensor("y_lo", [P, EC, TOK], F32R))
            ssm_conv(nc, io, cst, x_res, y_hi, y_lo)
            gqa(nc, io, cst, x_res, y_hi, y_lo)
        cached_qkv(nc, io, cst, x_res)
        cached_attention(nc, io, cst)
        output_ffn(nc, io, cst, x_res)


def kernel(**inputs):
    import concourse.bacc as bacc
    from concourse.bass_utils import run_bass_kernel_spmd

    nc = bacc.Bacc("TRN2", target_bir_lowering=False, num_devices=1)
    arrays, io = {}, {}
    for name, a in layouts(inputs).items():
        arrays[f"in_{name}"] = a
        io[name] = nc.dram_tensor(f"in_{name}", a.shape, mybir.dt.from_np(a.dtype), kind="ExternalInput").ap()
    io["out_t"] = nc.dram_tensor("out_t", (E, TOK), F32, kind="ExternalOutput").ap()
    build(nc, io)
    r = run_bass_kernel_spmd(nc, [arrays], core_ids=[0])
    return np.ascontiguousarray(r.results[0]["out_t"].T).reshape(B, S, E)
```

```python
from contextlib import ExitStack

import numpy as np

import concourse.bass as bass
from concourse import mybir

F32 = mybir.dt.float32
F32R = mybir.dt.float32r
I32 = mybir.dt.int32
ALU = mybir.AluOpType
ACT = mybir.ActivationFunctionType
X = mybir.AxisListType.X

P = 128
B, S, E = 32, 32, 512
TOK = B * S
EC = E // P
TT = TOK // P
HALF = TOK // 2
HQ, HK, D = 32, 8, 128
G = HQ // HK
N_MODES = 64
PAGES, PSIZE, NPP = 64, 32, 16
CACHE = NPP * PSIZE
KEYS = CACHE + S
SCALE = float(D) ** -0.5
THETA = 10000.0
EPS = 1e-6
LORA_N, RANK, LORA_SCALE = 8, 16, 2.0
BIG = 1e30
TWO_PI = 2.0 * np.pi
ROUND = 1.5 * 2.0 ** 23


def split_const(v, bits, n):
    parts = []
    for _ in range(n - 1):
        e = int(np.floor(np.log2(abs(v))))
        q = 2.0 ** (e - bits + 1)
        h = float(np.round(v / q) * q)
        parts.append(h)
        v -= h
    return parts + [float(v)]


PI2 = split_const(TWO_PI, 9, 3)
LN2 = split_const(float(np.log(2.0)), 12, 2)
EXP_TERMS = [1.0 / 5040, 1.0 / 720, 1.0 / 120, 1.0 / 24, 1.0 / 6, 0.5, 1.0]

I_STEPS, J_STEPS = 16, 32
ANG = 2 * I_STEPS + J_STEPS + 2
C_ID = 0
C_LSTEP = C_ID + P
C_SHIFT = C_LSTEP + ANG
C_RE = C_SHIFT + ANG
C_IM = C_RE + 1
C_LPOS = C_IM + 1
C_INVF = C_LPOS + EC
C_SPOS = C_INVF + D // 2
C_CAUSAL = C_SPOS + 1
C_KEYPOS = C_CAUSAL + S
C_PART = C_KEYPOS + KEYS
C_COLS = C_PART + 1


def constants():
    c = np.zeros((P, C_COLS), np.float32)
    p = np.arange(P)
    c[:, C_ID:C_ID + P] = np.eye(P)
    steps = np.concatenate([np.arange(I_STEPS) * J_STEPS, np.arange(I_STEPS) * J_STEPS, np.arange(J_STEPS), [1, 1]])
    c[:, C_LSTEP:C_LSTEP + ANG] = steps
    c[:, C_SHIFT:C_SHIFT + I_STEPS] = 0.25
    c[:64, C_SHIFT + 2 * I_STEPS:C_SHIFT + ANG - 2] = 0.25
    c[:, C_SHIFT + ANG - 2] = 0.25
    c[:64, C_RE] = 1
    c[64:, C_IM] = 1
    c[:, C_LPOS:C_LPOS + EC] = p[:, None] + P * np.arange(EC)
    c[:, C_INVF:C_INVF + D // 2] = np.float32(1.0) / np.float32(THETA) ** (np.arange(0, D, 2, dtype=np.float32) / np.float32(D))
    c[:, C_SPOS] = p % S
    c[:, C_CAUSAL:C_CAUSAL + S] = np.where(np.arange(S)[None, :] <= (p % S)[:, None], 0.0, -BIG)
    c[:, C_KEYPOS:C_KEYPOS + CACHE] = np.arange(CACHE)
    c[:, C_KEYPOS + CACHE:C_PART] = -BIG
    c[:, C_PART] = p
    return c


class Chain:

    def __init__(self, eng, sem):
        self.eng, self.sem, self.n = eng, sem, 0

    def __call__(self, instruction):
        self.n += 1
        instruction.then_inc(self.sem, 1)
        self.eng.wait_ge(self.sem, self.n)


def bc(ap, axis, shape):
    return ap.unsqueeze(axis).broadcast_to(shape)


def reduce_angle(step, v, ang, k, row_shift):
    step(v.scalar_tensor_tensor(out=k, in0=ang, scalar=1.0 / TWO_PI, in1=row_shift, op0=ALU.mult, op1=ALU.add))
    step(v.tensor_scalar(k, k, ROUND, ROUND, ALU.add, ALU.subtract))
    for part in PI2:
        step(v.scalar_tensor_tensor(out=ang, in0=k, scalar=-part, in1=ang, op0=ALU.mult, op1=ALU.add))
    step(v.scalar_tensor_tensor(out=ang, in0=row_shift, scalar=TWO_PI, in1=ang, op0=ALU.mult, op1=ALU.add))
    step(v.tensor_scalar(ang, ang, float(np.float32(3.1415925)), float(np.float32(-3.1415925)), ALU.min, ALU.max))


def accurate_exp(step, v, x, r, k, ki):
    step(v.tensor_scalar(x, x, -87.0, 88.0, ALU.max, ALU.min))
    step(v.tensor_scalar(k, x, 1.0 / float(np.log(2.0)), ROUND, ALU.mult, ALU.add))
    step(v.tensor_scalar(k, k, ROUND, None, ALU.subtract))
    step(v.scalar_tensor_tensor(out=r, in0=k, scalar=-LN2[0], in1=x, op0=ALU.mult, op1=ALU.add))
    step(v.scalar_tensor_tensor(out=r, in0=k, scalar=-LN2[1], in1=r, op0=ALU.mult, op1=ALU.add))
    step(v.tensor_scalar(x, r, EXP_TERMS[0], None, ALU.mult))
    for term in EXP_TERMS[1:]:
        step(v.scalar_tensor_tensor(out=x, in0=x, scalar=term, in1=r, op0=ALU.add, op1=ALU.mult))
    step(v.tensor_scalar(ki, k, 127.0, None, ALU.add))
    step(v.tensor_scalar(ki, ki, 23, None, ALU.logical_shift_left))
    step(v.scalar_tensor_tensor(out=x, in0=x, scalar=1.0, in1=ki.bitcast(F32), op0=ALU.add, op1=ALU.mult))


class Weights:

    def __init__(self, ctx, nc):
        self.raw = ctx.enter_context(nc.sbuf_tensor("w_raw", [P, 2, EC, 5 * D], F32))
        self.hi = ctx.enter_context(nc.sbuf_tensor("w_hi", [P, 2, EC, 5 * D], F32R))
        self.lo = ctx.enter_context(nc.sbuf_tensor("w_lo", [P, 2, EC, 5 * D], F32R))


def ssm_conv(nc, io, cst, x_res, y_hi, y_lo, weights):
    with ExitStack() as ctx:
        sb = lambda name, shape, dt=F32: ctx.enter_context(nc.sbuf_tensor(name, shape, dt))
        ps = lambda name, shape: ctx.enter_context(nc.psum_tensor(name, shape, F32))
        sem = lambda name: ctx.enter_context(nc.semaphore(name))
        modes = sb("modes", [P, 5, B])
        expo = sb("expo", [P, 3, B])
        tmp = sb("tmp", [P, 10, B])
        ratio = sb("ratio", [P, 6, B])
        tmpi = sb("tmpi", [P, 3, B], I32)
        ang = sb("ang", [P, B, ANG])
        turns = sb("turns", [P, B, ANG])
        mag = sb("mag", [P, B, ANG])
        coef = sb("coef", [P, B, I_STEPS])
        coef2 = sb("coef2", [P, B, I_STEPS])
        kern = sb("kern", [I_STEPS, B, J_STEPS])
        skip_row = sb("skip_row", [1, B])
        zeros = sb("zeros", [B, P])
        u_rev = sb("u_rev", [P, EC, S, B])
        toep = sb("toep", [P, 4, E])
        len_i = sb("len_i", [P, B], I32)
        len_f = sb("len_f", [P, B])
        keep = sb("keep", [P, EC, B])
        y = sb("y", [P, EC, B, S])
        p_kern = ps("p_kern", [I_STEPS, B * J_STEPS])
        p_conv = ps("p_conv", [P, 2, 4, EC, B])

        log_in = sem("log_in")
        par_in = sem("par_in")
        row_in = sem("row_in")
        decay_ready = sem("decay_ready")
        mag_ready = sem("mag_ready")
        pool_step = sem("pool_step_conv")
        norm_ready = sem("norm_ready")
        ratio_ready = sem("ratio_ready")
        u_in = sem("u_in")
        dve_step = sem("dve_step_conv")
        act_step = sem("act_step_conv")
        angles_ready = sem("angles_ready")
        sines_ready = sem("sines_ready")
        coef_ready = sem("coef_ready")
        kern_done = sem("kern_done")
        kern_ready = sem("kern_ready")
        kern_out = sem("kern_out")
        toep_in = [sem(f"toep_in{i}") for i in range(4)]
        conv_done = sem("conv_done")
        y_ready = sem("y_ready")
        conv_taken = sem("conv_taken")
        split_done = sem("split_done")
        v_weights_in = sem("v_weights_in")
        v_weights_hi = sem("v_weights_hi")
        v_weights_lo = sem("v_weights_lo")
        hi_ready = sem("hi_ready")
        d_re, d_im = tmp[:, 4, :], tmp[:, 5, :]
        lstep = bc(cst[:, C_LSTEP:C_LSTEP + ANG], 1, [P, B, ANG])
        shift = bc(cst[:, C_SHIFT:C_SHIFT + ANG], 1, [P, B, ANG])
        y_flat = y[:, :, :, :].rearrange("p c b s -> p c (b s)")
        four_heads = lambda a, q: a.rearrange("p c (b s) -> p (c b) s", s=S)[:, :, 4 * q:4 * q + 4]
        kpad = io["kpad"]
        kp_rows = kpad.rearrange("(h m) -> h m", h=S)

        block = ctx.enter_context(nc.Block())

        @block.sync
        def _(sp):
            sp.dma_start(modes[:, 0, :], io["log_dt_b"].partition_broadcast(P)).then_inc(log_in, 16)
            for i, name, done in ((1, "log_A_real_t", log_in), (2, "A_imag_t", par_in), (3, "C_re_t", par_in), (4, "C_im_t", par_in)):
                for half in range(2):
                    sp.dma_start(modes[64 * half:64 * half + 64, i, :], io[name]).then_inc(done, 16)
                if i == 2:
                    sp.dma_start(cst[:, :], io["cst"]).then_inc(par_in, 16)
            sp.dma_start(skip_row[:, :], io["D"].rearrange("(o h) -> o h", o=1)).then_inc(row_in, 16)
            sp.dma_start(len_i[:, :], io["length"].partition_broadcast(P)).then_inc(row_in, 16)
            sp.dma_start(u_rev[:, :, :, :].rearrange("p c s b -> p c (s b)"),
                         io["u_rev"].rearrange("(c p) n -> p c n", p=P)).then_inc(u_in, 16)
            sp.dma_start(x_res[:, :, :], io["xT"].rearrange("(c p) n -> p c n", p=P)).then_inc(u_in, 16)
            w_qkv = io["w_qkv_t"].rearrange("(c p) n -> p c n", p=P)
            for n in range(2):
                at = (HQ + HK) * D + n * E
                sp.dma_start(weights.raw[:, n, :, 0:E], w_qkv[:, :, at:at + E]).then_inc(v_weights_in, 16)
            sp.wait_ge(kern_ready, 1)
            sp.dma_start(kp_rows[:, 0:P], zeros[:, :]).then_inc(kern_out, 16)
            sp.dma_start(kp_rows[:, P:P + E].rearrange("h (i j) -> i h j", i=I_STEPS), kern[:, :, :]).then_inc(kern_out, 16)
            sp.wait_ge(kern_out, 32)

            def load(s_at, slot):
                win = kpad[bass.ds(s_at * (P + E) + 1, P + E - 1)]
                win = bass.AP(tensor=win.tensor, offset=win.offset, ap=[[1, P], [1, E]])
                sp.dma_start(toep[:, slot, :], win).then_inc(toep_in[slot], 16)

            for s in range(S):
                if s >= 4:
                    sp.wait_ge(conv_done, s - 3)
                load(s, s % 4)
            sp.wait_ge(u_in, 32)

        @block.gpsimd
        def _(pool):
            step = Chain(pool, pool_step)
            tt = nc.gpsimd.tensor_tensor
            pool.wait_ge(decay_ready, 1)
            tt(mag[:, :, :], bc(d_re, 2, [P, B, ANG]), lstep, ALU.mult).then_inc(mag_ready, 1)
            n_re, n_im, norm, t0, t1 = (ratio[:, i, :] for i in range(5))
            a_re, aim, c_re, c_im = tmp[:, 6, :], modes[:, 2, :], modes[:, 3, :], modes[:, 4, :]
            pool.wait_ge(par_in, 16 * 7)
            step(tt(t0, a_re, a_re, ALU.mult))
            step(tt(t1, aim, aim, ALU.mult))
            step(tt(norm, t0, t1, ALU.add))
            pool.engine_nop().then_inc(norm_ready, 1)
            step(tt(t0, c_re, a_re, ALU.mult))
            step(tt(t1, c_im, aim, ALU.mult))
            step(tt(n_re, t0, t1, ALU.add))
            step(tt(t0, c_im, a_re, ALU.mult))
            step(tt(t1, c_re, aim, ALU.mult))
            tt(n_im, t0, t1, ALU.subtract).then_inc(ratio_ready, 1)
            for n in range(2):
                pool.wait_ge(v_weights_hi, n + 1)
                nc.gpsimd.tensor_tensor(weights.lo[:, n, :, 0:E], weights.raw[:, n, :, 0:E],
                                        weights.hi[:, n, :, 0:E].bitcast(F32), ALU.subtract).then_inc(v_weights_lo, 1)

        @block.scalar
        def _(act):
            act.wait_ge(v_weights_in, 32)
            for n in range(2):
                nc.scalar.activation(weights.hi[:, n, :, 0:E], weights.raw[:, n, :, 0:E], ACT.Copy).then_inc(v_weights_hi, 1)
            act.wait_ge(mag_ready, 1)
            nc.scalar.activation(mag[:, :, :], mag[:, :, :], ACT.Exp).then_inc(act_step, 1)
            act.wait_ge(angles_ready, 1)
            nc.scalar.activation(ang[:, :, :], ang[:, :, :], ACT.Sin).then_inc(sines_ready, 1)
            for q in range(S // 4):
                act.wait_ge(y_ready, q + 1)
                nc.scalar.activation(four_heads(y_hi[:, :, :], q), four_heads(y_flat, q), ACT.Copy).then_inc(hi_ready, 1)

        @block.vector
        def _(v):
            step = Chain(v, dve_step)
            step(v.memset(zeros[:, :], 0.0))
            v.wait_ge(log_in, 16 * 3)
            step(v.tensor_copy(expo[:, 0:2, :], modes[:, 0:2, :]))
            accurate_exp(step, v, expo[:, 0:2, :], tmp[:, 0:2, :], tmp[:, 2:4, :], tmpi[:, 0:2, :])
            dt, ea, aim = expo[:, 0, :], expo[:, 1, :], modes[:, 2, :]
            a_re = tmp[:, 6, :]
            step(v.tensor_scalar(a_re, ea, -1.0, None, ALU.mult))
            step(v.tensor_tensor(d_re, a_re, dt, ALU.mult))
            v.wait_ge(par_in, 16 * 7)
            v.tensor_tensor(d_im, aim, dt, ALU.mult).then_inc(decay_ready, 1)
            v.wait_ge(decay_ready, 1)
            step(v.tensor_tensor(ang[:, :, :], bc(d_im, 2, [P, B, ANG]), lstep, ALU.mult))
            reduce_angle(step, v, ang[:, :, :], turns[:, :, :], shift)
            v.tensor_copy(expo[:, 2, :], d_re).then_inc(angles_ready, 1)
            v.wait_ge(angles_ready, 1)
            accurate_exp(step, v, expo[:, 2, :], tmp[:, 0, :], tmp[:, 1, :], tmpi[:, 2, :])
            e_re, e_im, t0, t1 = tmp[:, 0, :], tmp[:, 1, :], tmp[:, 2, :], tmp[:, 3, :]
            inv, q_re, q_im = tmp[:, 9, :], ratio[:, 5, :], ratio[:, 2, :]
            v.wait_ge(norm_ready, 1)
            step(v.reciprocal(inv, ratio[:, 2, :]))
            v.wait_ge(ratio_ready, 1)
            step(v.tensor_tensor(q_re, ratio[:, 0, :], inv, ALU.mult))
            step(v.tensor_tensor(q_im, ratio[:, 1, :], inv, ALU.mult))
            v.wait_ge(sines_ready, 1)
            v.wait_ge(act_step, 1)
            step(v.tensor_tensor(e_re, expo[:, 2, :], ang[:, :, ANG - 2], ALU.mult))
            step(v.tensor_tensor(e_im, expo[:, 2, :], ang[:, :, ANG - 1], ALU.mult))
            step(v.tensor_scalar(e_re, e_re, -1.0, None, ALU.add))
            n_re, n_im, ct_re, ct_im = tmp[:, 7, :], tmp[:, 8, :], ratio[:, 0, :], ratio[:, 1, :]
            step(v.tensor_tensor(t0, q_re, e_re, ALU.mult))
            step(v.tensor_tensor(t1, q_im, e_im, ALU.mult))
            step(v.tensor_tensor(ct_re, t0, t1, ALU.subtract))
            step(v.tensor_tensor(t0, q_re, e_im, ALU.mult))
            step(v.tensor_tensor(t1, q_im, e_re, ALU.mult))
            step(v.tensor_tensor(ct_im, t0, t1, ALU.add))
            re_row, im_row = cst[:, C_RE:C_RE + 1], cst[:, C_IM:C_IM + 1]
            alpha, beta = n_re, n_im
            step(v.tensor_scalar(t0, ct_re, re_row, 2.0, ALU.mult, ALU.mult))
            step(v.tensor_scalar(t1, ct_im, im_row, -2.0, ALU.mult, ALU.mult))
            step(v.tensor_tensor(alpha, t0, t1, ALU.add))
            step(v.tensor_scalar(t0, ct_im, re_row, -2.0, ALU.mult, ALU.mult))
            step(v.tensor_scalar(t1, ct_re, im_row, -2.0, ALU.mult, ALU.mult))
            step(v.tensor_tensor(beta, t0, t1, ALU.add))
            step(v.tensor_tensor(ang[:, :, :], ang[:, :, :], mag[:, :, :], ALU.mult))
            step(v.tensor_tensor(coef[:, :, :], ang[:, :, 0:I_STEPS], bc(alpha, 2, [P, B, I_STEPS]), ALU.mult))
            step(v.tensor_tensor(coef2[:, :, :], ang[:, :, I_STEPS:2 * I_STEPS], bc(beta, 2, [P, B, I_STEPS]), ALU.mult))
            v.tensor_tensor(coef[:, :, :], coef[:, :, :], coef2[:, :, :], ALU.add).then_inc(coef_ready, 1)
            v.wait_ge(row_in, 32)
            step(v.tensor_copy(len_f[:, :], len_i[:, :]))
            for c in range(EC):
                step(v.tensor_scalar(keep[:, c, :], len_f[:, :], cst[:, C_LPOS + c:C_LPOS + c + 1], None, ALU.is_gt))
            v.wait_ge(kern_done, 1)
            step(v.tensor_copy(kern[:, :, :].rearrange("i h j -> i (h j)"), p_kern[:, :]))
            v.tensor_tensor(kern[0:1, :, 0], kern[0:1, :, 0], skip_row[:, :], ALU.add).then_inc(kern_ready, 1)
            def split_low(q):
                v.wait_ge(hi_ready, q + 1)
                v.tensor_tensor(four_heads(y_lo[:, :, :], q), four_heads(y_flat, q), four_heads(y_hi[:, :, :], q).bitcast(F32),
                                ALU.subtract).then_inc(split_done, 1)

            for q in range(S // 4):
                v.wait_ge(conv_done, 4 * q + 4)
                for c in range(EC):
                    last = v.tensor_tensor(y[:, c, :, 4 * q:4 * q + 4].rearrange("p b s -> p s b"),
                                           p_conv[:, q % 2, :, c, :],
                                           bc(keep[:, c, :], 1, [P, 4, B]), ALU.mult)
                last.then_inc(y_ready, 1)
                if q >= 1:
                    split_low(q - 1)
            split_low(S // 4 - 1)

        @block.tensor
        def _(pe):
            pe.wait_ge(coef_ready, 1)
            for h in range(S):
                last = pe.matmul(p_kern[:, h * J_STEPS:(h + 1) * J_STEPS], coef[:, h, :],
                                 ang[:, h, 2 * I_STEPS:2 * I_STEPS + J_STEPS], start=True, stop=True)
            last.then_inc(kern_done, 1)
            pe.wait_ge(u_in, 32)
            for s in range(S):
                if s % 4 == 0 and s >= 8:
                    pe.wait_ge(y_ready, s // 4 - 1)
                pe.wait_ge(toep_in[s % 4], 16 * (s // 4 + 1))
                for d in range(EC):
                    last = pe.matmul(p_conv[:, s // 4 % 2, s % 4, d:EC, :], toep[:, s % 4, d * P:(d + 1) * P],
                                     u_rev[:, 0:EC - d, s, :], start=(d == 0 and s % 4 == 0), stop=(d == EC - 1),
                                     skip_group_check=True)
                last.then_inc(conv_done, 1)


def three_pass(pe, out, a_hi, a_lo, b_hi, b_lo, start, stop):
    pe.matmul(out, a_hi, b_hi, start=start, stop=False)
    pe.matmul(out, a_hi, b_lo, start=False, stop=False)
    return pe.matmul(out, a_lo, b_hi, start=False, stop=stop)


def gqa(nc, io, cst, x_res, y_hi, y_lo, weights):
    with ExitStack() as ctx:
        sb = lambda name, shape, dt=F32: ctx.enter_context(nc.sbuf_tensor(name, shape, dt))
        sem = lambda name: ctx.enter_context(nc.semaphore(name))
        w_raw, w_hi, w_lo = weights.raw[:, 0], weights.hi[:, 0], weights.lo[:, 0]
        wd_raw, wd_hi, wd_lo = (a[:, 1, :, 0:E] for a in (weights.raw, weights.hi, weights.lo))
        q_t = sb("q_t", [P, B, G, S])
        k_t = sb("k_t", [P, TOK])
        o_hi = sb("o_hi", [P, G, TOK], F32R)
        o_lo = sb("o_lo", [P, G, TOK], F32R)
        v_nat = sb("v_nat", [P, TT, D])
        v_out = sb("v_out", [P, 2, E])
        probs = sb("probs", [P, 2, B // 2, S])
        probs_t = sb("probs_t", [P, 2, 4, P])
        top = sb("top", [P, 2, B // 2])
        total = sb("total", [P, 2, B // 2])
        p_proj = ctx.enter_context(nc.psum_tensor("p_proj", [P, 2, E], F32))
        p_score = ctx.enter_context(nc.psum_tensor("p_score", [P, 2, 4, P], F32))
        p_val = ctx.enter_context(nc.psum_tensor("p_val", [P, 4, 4, P], F32))
        ident = cst[:, C_ID:C_ID + P]
        causal = cst[:, C_CAUSAL:C_CAUSAL + S]

        w_in = sem("w_in")
        w_hi_ready = sem("w_hi_ready")
        w_lo_ready = sem("w_lo_ready")
        wd_in = sem("wd_in")
        wd_hi_ready = sem("wd_hi_ready")
        wd_lo_ready = sem("wd_lo_ready")
        proj_done = sem("proj_done")
        proj_taken = sem("proj_taken")
        v_stored = [sem(f"v_stored{i}") for i in range(2)]
        v_in = sem("v_in")
        w_next_in = sem("w_next_in")
        x_hi_ready = sem("x_hi_ready")
        x_lo_ready = sem("x_lo_ready")
        scores_done = sem("scores_done")
        masked = sem("masked")
        top_ready = sem("top_ready")
        centred = sem("centred")
        exp_done = sem("exp_done")
        total_ready = sem("total_ready")
        inverse_ready = sem("inverse_ready")
        probs_ready = sem("probs_ready")
        turned = sem("turned")
        turned_taken = sem("turned_taken")
        val_done = sem("val_done")
        o_hi_ready = sem("o_hi_ready")
        o_lo_ready = sem("o_lo_ready")
        out_done = sem("out_done")
        out_added = sem("out_added")

        NV = 2
        VT = NV * TT
        QT = 2 * (G + 1)
        OT = 2 * EC
        w_qkv = io["w_qkv_t"].rearrange("(c p) n -> p c n", p=P)
        w_dense = io["w_dense_t"].rearrange("(m p) n -> p m n", p=P)
        w_next = io["w_vkq_t"].rearrange("(c p) n -> p c n", p=P)
        v_rows = io["v_attn"].rearrange("(t p) n -> p t n", p=P)
        heads = lambda body, eng: (body(0, True, False), _loop(eng, 1, HK - 1, lambda k: body(k, False, False)),
                                   body(HK - 1, False, True))

        pick = lambda o, hf, j: o[:, :, :].rearrange("p g (hf bg j s) -> p hf j bg g s", hf=2, j=4, s=S)[:, hf, j]

        block = ctx.enter_context(nc.Block())

        @block.sync
        def _(sp):
            sp.dma_start(w_raw[:, :, 0:E], w_qkv[:, :, 0:E]).then_inc(w_in, 16)
            sp.dma_start(w_raw[:, :, E:5 * D], w_qkv[:, :, HQ * D:HQ * D + D]).then_inc(w_in, 16)
            sp.dma_start(wd_raw[:, :, :], w_dense[:, 0:G, :]).then_inc(wd_in, 16)
            for t in range(VT):
                sp.wait_ge(proj_taken, t + 1)
                sp.dma_start(v_rows[:, t % TT, t // TT * E:(t // TT + 1) * E], v_out[:, t % 2, :]).then_inc(v_stored[t % 2], 16)
            for i in range(2):
                sp.wait_ge(v_stored[i], 16 * VT // 2)

            def body(k, first, last):
                q_col, k_col, v_col = sp.snap(k * (G * D) + G * D), sp.snap(k * D + (HQ + 1) * D), sp.snap(k * D)
                d_row = sp.snap(k * G + G)
                if not first:
                    sp.wait_ge(val_done, 2 * k)
                sp.dma_start(v_nat[:, :, :], v_rows[:, :, bass.ds(v_col, D)]).then_inc(v_in, 16)
                if not last:
                    sp.wait_ge(w_lo_ready, k + 1)
                    sp.dma_start(w_raw[:, :, 0:E], w_qkv[:, :, bass.ds(q_col, E)]).then_inc(w_in, 16)
                    sp.dma_start(w_raw[:, :, E:5 * D], w_qkv[:, :, bass.ds(k_col, D)]).then_inc(w_in, 16)
                    sp.wait_ge(wd_lo_ready, k + 1)
                    sp.dma_start(wd_raw[:, :, :], w_dense[:, bass.ds(d_row, G), :]).then_inc(wd_in, 16)

            heads(body, sp)
            for slot, used in ((0, w_lo_ready), (1, wd_lo_ready)):
                sp.wait_ge(used, HK)
                sp.dma_start(weights.raw[:, slot, :, 0:E], w_next[:, :, slot * E:(slot + 1) * E]).then_inc(w_next_in, 16)
            sp.wait_ge(w_next_in, 32)

        @block.scalar
        def _(act):
            def split_w(k):
                act.wait_ge(w_in, 32 * k + 32)
                act.wait_ge(proj_done, TT if isinstance(k, int) and k == 0 else k * QT + VT)
                nc.scalar.activation(w_hi[:, :, :], w_raw[:, :, :], ACT.Copy).then_inc(w_hi_ready, 1)

            for t in range(VT):
                if t == TT + 1:
                    split_w(0)
                act.wait_ge(proj_done, t + 1)
                if t >= 2:
                    act.wait_ge(v_stored[t % 2], 16 * (t // 2))
                nc.scalar.activation(v_out[:, t % 2, :], p_proj[:, t % 2, :], ACT.Copy).then_inc(proj_taken, 1)

            def copy_turned(k, hf):
                act.wait_ge(turned, 2 * k + hf + 1)
                nc.scalar.activation(probs_t[:, hf, :, :], p_score[:, hf, :, :], ACT.Copy).then_inc(turned_taken, 1)

            def exponentials(k, hf):
                act.wait_ge(centred, 2 * k + hf + 1)
                nc.scalar.activation(probs[:, hf, :, :], probs[:, hf, :, :], ACT.Exp).then_inc(exp_done, 1)

            def split_values(k, hf):
                act.wait_ge(val_done, 2 * k + hf + 1)
                for j in range(4):
                    nc.scalar.activation(pick(o_hi, hf, j), p_val[:, j, :, :].rearrange("p bg (g s) -> p bg g s", s=S),
                                         ACT.Copy).then_inc(o_hi_ready, 1)

            def body(k, first, last):
                for i in range(QT):
                    act.wait_ge(proj_done, k * QT + VT + i + 1)
                    hf, head = i // (G + 1), i % (G + 1)
                    if head < G:
                        to = q_t[:, hf * B // 2:(hf + 1) * B // 2, head, :]
                    else:
                        to = k_t[:, hf * HALF:(hf + 1) * HALF].rearrange("p (b s) -> p b s", s=S)
                    nc.scalar.activation(to, p_proj[:, i % 2, :].rearrange("p (b s) -> p b s", s=S), ACT.Copy).then_inc(proj_taken, 1)
                exponentials(k, 0)
                if not last:
                    split_w(k + 1)
                copy_turned(k, 0)
                exponentials(k, 1)
                split_values(k, 0)
                copy_turned(k, 1)
                act.wait_ge(wd_in, 16 * k + 16)
                if not first:
                    act.wait_ge(out_done, k * OT)
                else:
                    act.wait_ge(proj_done, VT)
                nc.scalar.activation(wd_hi[:, :, :], wd_raw[:, :, :], ACT.Copy).then_inc(wd_hi_ready, 1)
                split_values(k, 1)

            heads(body, act)
            act.wait_ge(w_next_in, 32)
            act.wait_ge(proj_done, VT + HK * QT)
            nc.scalar.activation(w_hi[:, :, 0:E], w_raw[:, :, 0:E], ACT.Copy).then_inc(w_hi_ready, 1)
            for i in range(OT):
                act.wait_ge(out_added, (HK - 1) * OT + i + 2)
                at = slice(i // EC * HALF, (i // EC + 1) * HALF)
                nc.scalar.activation(y_hi[:, i % EC, at], x_res[:, i % EC, at], ACT.Copy).then_inc(x_hi_ready, 1)

        @block.gpsimd
        def _(pool):
            def split_lo(k):
                pool.wait_ge(w_hi_ready, k + 1)
                nc.gpsimd.tensor_tensor(w_lo[:, :, :], w_raw[:, :, :], w_hi[:, :, :].bitcast(F32), ALU.subtract).then_inc(w_lo_ready, 1)

            split_lo(0)

            def body(k, first, last):
                if not last:
                    split_lo(k + 1)
                pool.wait_ge(wd_hi_ready, k + 1)
                nc.gpsimd.tensor_tensor(wd_lo[:, :, :], wd_raw[:, :, :], wd_hi[:, :, :].bitcast(F32), ALU.subtract).then_inc(wd_lo_ready, 1)

            heads(body, pool)
            pool.wait_ge(w_hi_ready, HK + 1)
            nc.gpsimd.tensor_tensor(w_lo[:, :, 0:E], w_raw[:, :, 0:E], w_hi[:, :, 0:E].bitcast(F32), ALU.subtract).then_inc(w_lo_ready, 1)

        @block.vector
        def _(v):
            def centre(k, hf):
                n = 2 * k + hf + 1
                v.wait_ge(scores_done, n)
                v.scalar_tensor_tensor(out=probs[:, hf, :, :], in0=p_score[:, hf, :, :].rearrange("p a (b t) -> p (a b) t", t=S),
                                       scalar=SCALE, in1=bc(causal, 1, [P, B // 2, S]), op0=ALU.mult, op1=ALU.add).then_inc(masked, 1)
                v.wait_ge(masked, n)
                v.tensor_reduce(top[:, hf, :], probs[:, hf, :, :], X, ALU.max).then_inc(top_ready, 1)
                v.wait_ge(top_ready, n)
                v.tensor_tensor(probs[:, hf, :, :], probs[:, hf, :, :], bc(top[:, hf, :], 2, [P, B // 2, S]),
                                ALU.subtract).then_inc(centred, 1)

            def normalise(k, hf):
                n = 2 * k + hf + 1
                v.wait_ge(exp_done, n)
                v.tensor_reduce(total[:, hf, :], probs[:, hf, :, :], X, ALU.add).then_inc(total_ready, 1)
                v.wait_ge(total_ready, n)
                v.reciprocal(total[:, hf, :], total[:, hf, :]).then_inc(inverse_ready, 1)
                v.wait_ge(inverse_ready, n)
                v.tensor_tensor(probs[:, hf, :, :], probs[:, hf, :, :], bc(total[:, hf, :], 2, [P, B // 2, S]),
                                ALU.mult).then_inc(probs_ready, 1)

            def add_out(k, i):
                v.wait_ge(out_done, k * OT + i + 1)
                at = x_res[:, i % EC, i // EC * HALF:(i // EC + 1) * HALF]
                v.tensor_tensor(at, at, p_proj[:, i % 2, :], ALU.add).then_inc(out_added, 1)

            def split_values(k, hf):
                for j in range(4):
                    v.wait_ge(o_hi_ready, 8 * k + 4 * hf + j + 1)
                    v.tensor_tensor(pick(o_lo, hf, j), p_val[:, j, :, :].rearrange("p bg (g s) -> p bg g s", s=S),
                                    pick(o_hi, hf, j).bitcast(F32), ALU.subtract).then_inc(o_lo_ready, 1)

            def body(k, first, last):
                add = (lambda i: None) if first else (lambda i: add_out(k - 1, i))
                centre(k, 0)
                add(0)
                normalise(k, 0)
                add(1)
                add(2)
                centre(k, 1)
                add(3)
                split_values(k, 0)
                normalise(k, 1)
                for i in range(EC, OT):
                    add(i)
                split_values(k, 1)

            v.memset(top[:, :, :], 0.0).then_inc(out_added, 1)
            heads(body, v)
            def split_x(i):
                v.wait_ge(x_hi_ready, i + 1)
                at = slice(i // EC * HALF, (i // EC + 1) * HALF)
                v.tensor_tensor(y_lo[:, i % EC, at], x_res[:, i % EC, at], y_hi[:, i % EC, at].bitcast(F32), ALU.subtract).then_inc(x_lo_ready, 1)

            for i in range(OT):
                add_out(HK - 1, i)
                if i >= 1:
                    split_x(i - 1)
            split_x(OT - 1)

        @block.tensor
        def _(pe):
            for t in range(VT):
                if t >= 2:
                    pe.wait_ge(proj_taken, t - 1)
                for c in range(EC):
                    at = slice(t % TT * P, (t % TT + 1) * P)
                    last_mm = three_pass(pe, p_proj[:, t % 2, :], y_hi[:, c, at], y_lo[:, c, at],
                                         weights.hi[:, t // TT, c, 0:E], weights.lo[:, t // TT, c, 0:E],
                                         c == 0, c == EC - 1)
                last_mm.then_inc(proj_done, 1)

            def product_tile(k, i, among, final=False):
                if i == 0:
                    pe.wait_ge(wd_lo_ready, k + 1)
                if i % EC == 0:
                    pe.wait_ge(o_lo_ready, 8 * k + 4 * (i // EC) + 4)
                if i < 2 and not final:
                    pe.wait_ge(proj_taken, (k + 1) * QT + VT + QT - 1 + i)
                else:
                    pe.wait_ge(out_added, k * OT + i)
                to = slice(i % EC * P, (i % EC + 1) * P)
                at = slice(i // EC * HALF, (i // EC + 1) * HALF)
                for g in range(G):
                    last_mm = three_pass(pe, p_proj[:, i % 2, :], wd_hi[:, g, to], wd_lo[:, g, to],
                                         o_hi[:, g, at], o_lo[:, g, at], g == 0, g == G - 1)
                    if g == G - 1:
                        last_mm.then_inc(out_done, 1)
                    among(g)

            def score(k, hf, n, first):
                if n == 0 and not first:
                    pe.wait_ge(turned_taken, 2 * k + hf - 1)
                b = hf * B // 2 + n
                mm = pe.matmul(p_score[:, hf, n // 4, n % 4 * S:(n % 4 + 1) * S], q_t[:, b, :, :].rearrange("p g s -> p (g s)"),
                               k_t[:, b * S:(b + 1) * S], start=True, stop=True)
                if n == B // 2 - 1:
                    mm.then_inc(scores_done, 1)

            def transposes(k, hf):
                pe.wait_ge(probs_ready, 2 * k + hf + 1)
                for bg in range(4):
                    mm = pe.transpose(p_score[:, hf, bg, :], probs[:, hf, 4 * bg:4 * bg + 4, :].rearrange("p b t -> p (b t)"), ident)
                mm.then_inc(turned, 1)

            def values(k, hf, first):
                if hf == 0:
                    pe.wait_ge(v_in, 16 * k + 16)
                pe.wait_ge(turned_taken, 2 * k + hf + 1)
                if not (first and hf == 0):
                    pe.wait_ge(o_lo_ready, 8 * k + 4 * hf)
                for n in range(B // 2):
                    bg, j = n // 4, n % 4
                    rows = slice(S * j, S * j + S)
                    mm = pe.matmul(p_val[:, j, bg, :], v_nat[rows, hf * 4 + bg, :], probs_t[rows, hf, bg, :],
                                   start=True, stop=True)
                mm.then_inc(val_done, 1)

            def body(k, first, last):
                pe.wait_ge(w_lo_ready, k + 1)
                if not first:
                    pe.wait_ge(out_added, k * OT - OT + 1)
                for i in range(QT):
                    hf, head = i // (G + 1), i % (G + 1)
                    pe.wait_ge(proj_taken, k * QT + VT + i - 1)
                    at = slice(hf * HALF, (hf + 1) * HALF)
                    m = slice(head * D, (head + 1) * D)
                    for c in range(EC):
                        last_mm = three_pass(pe, p_proj[:, i % 2, :], w_hi[:, c, m], w_lo[:, c, m],
                                             y_hi[:, c, at], y_lo[:, c, at], c == 0, c == EC - 1)
                        if c == EC - 1:
                            last_mm.then_inc(proj_done, 1)
                        if i > G + 1:
                            score(k, 0, (i - G - 2) * EC + c, first)
                if first:
                    pe.wait_ge(proj_taken, k * QT + VT + QT)
                    for n in range(B // 2):
                        score(k, 1, n, first)
                    for hf in range(2):
                        transposes(k, hf)
                        values(k, hf, first)
                    return
                for i in range(OT):
                    hf = i // EC

                    def among(g):
                        if 0 < i < EC:
                            n = (i - 1) * (G + 1) + g + min(g, 1)
                            for n in ((n, n + 1) if g == 0 else (n,)):
                                score(k, 1, n, first)
                            if i == EC - 1 and g == G - 1:
                                score(k, 1, B // 2 - 1, first)

                    if i % EC == EC - 1:
                        transposes(k, hf)
                    product_tile(k - 1, i, among)
                    if i % EC == EC - 1:
                        values(k, hf, first)

            heads(body, pe)
            for i in range(OT):
                product_tile(HK - 1, i, lambda g: None, final=True)


def _loop(eng, start, end, body):
    with eng.Fori(start, end) as i:
        body(i)


QKV_CHUNKS = (HQ + 2 * HK) * D // E
LAG = 3


def cached_qkv(nc, io, cst, x_hi, x_lo, weights):
    with ExitStack() as ctx:
        sb = lambda name, shape, dt=F32: ctx.enter_context(nc.sbuf_tensor(name, shape, dt))
        sem = lambda name: ctx.enter_context(nc.semaphore(name))
        w_raw, w_hi, w_lo = (a[:, :, :, 0:E] for a in (weights.raw, weights.hi, weights.lo))
        len_i = sb("len3_i", [P, TT], I32)
        pos = sb("pos", [P, TT])
        quarter = sb("quarter", [P, 2])
        ang = sb("ang3", [P, 2, TT, D // 2])
        turns = sb("turns3", [P, 2, TT, D // 2])
        norm_w = sb("norm_w", [P, 2, D])
        rot = sb("rot", [P, 2, 2, TT, D])
        squares = sb("squares", [P, 4, 4])
        rms = sb("rms", [P, 4, 4])
        eps = sb("eps", [P, 1])
        inv_rms = sb("inv_rms", [P, 4, 4])
        normed = sb("normed", [P, 4, 4, D])
        part_a = sb("part_a", [P, 4, 4, D])
        part_b = sb("part_b", [P, 4, 4, D])
        stage = sb("stage", [P, 4, 4, 4, S])
        v_out = sb("v3_out", [P, 2, E])
        p_tile = ctx.enter_context(nc.psum_tensor("p_tile", [P, 4, E], F32))
        p_turn = ctx.enter_context(nc.psum_tensor("p_turn", [P, 2, 4, P], F32))
        ident = cst[:, C_ID:C_ID + P]

        len_in = sem("len_in")
        w_in = [sem(f"w3_in{i}") for i in range(2)]
        step_s = sem("rot_step")
        angles3 = sem("angles3")
        sines3 = sem("sines3")
        hi_piece = sem("hi_piece")
        lo_piece = sem("lo_piece")
        tile_done = sem("tile_done")
        tile_taken = sem("tile_taken")
        v_stored = [sem(f"v3_stored{i}") for i in range(2)]
        squares_ready = sem("squares_ready")
        rms_ready = sem("rms_ready")
        inv_ready = sem("inv_ready")
        a_ready = sem("a_ready")
        b_ready = sem("b_ready")
        rotated = sem("rotated")
        half_rotated = sem("half_rotated")
        turned = sem("turned3")
        staged = sem("staged")
        stored = [sem(f"stored{i}") for i in range(4)]

        w_all = io["w_vkq_t"].rearrange("(c p) n -> p c n", p=P)
        v_rows = io["v_new"].rearrange("(t p) n -> p t n", p=P)
        qk = io["qk_new"]
        PAIR = 2 * TT
        PAIRS = QKV_CHUNKS // 2
        pairs = lambda body, eng: (body(1, True, False), _loop(eng, 2, PAIRS - 1, lambda m: body(m, False, False)),
                                   body(PAIRS - 1, False, True))

        block = ctx.enter_context(nc.Block())

        @block.sync
        def _(sp):
            for bq in range(4):
                src = io["cache_len"].rearrange("(t q) -> q t", q=4)[bq]
                sp.dma_start(len_i[S * bq:S * bq + S, :], src.partition_broadcast(S), allow_slow_non_contiguous=True).then_inc(len_in, 16)
            sp.dma_start(norm_w[:, 0, :], io["q_norm"].partition_broadcast(P)).then_inc(len_in, 16)
            sp.dma_start(norm_w[:, 1, :], io["k_norm"].partition_broadcast(P)).then_inc(len_in, 16)

            def load_w(n, slot, col):
                if not (isinstance(n, int) and n == 2):
                    sp.wait_ge(lo_piece, (n - 2) * EC)
                sp.dma_start(w_raw[:, slot, :, :], w_all[:, :, bass.ds(col, E)]).then_inc(w_in[slot], 16)

            for t in range(PAIR):
                if t % TT == 4:
                    load_w(t // TT + 2, t // TT, (t // TT + 2) * E)
                sp.wait_ge(tile_taken, t + 1)
                sp.dma_start(v_rows[:, t % TT, t // TT * E:(t // TT + 1) * E], v_out[:, t % 2, :]).then_inc(v_stored[t % 2], 16)

            def body(m, first, last):
                cols = [sp.snap((2 * m + 2 + i) * E) for i in range(2)]
                to = [sp.snap((2 * m - 2 + i) * P) for i in range(2)]
                for i in range(PAIR):
                    if i % TT == 4 and not last:
                        load_w(2 * m + 2 + i // TT, i // TT, cols[i // TT])
                    sp.wait_ge(staged, (m - 1) * PAIR + i + 1)
                    b0 = i % TT * 4
                    sp.dma_start(qk[b0:b0 + 4, :, bass.ds(to[i // TT], P)].rearrange("b d n -> d b n"),
                                 stage[:, i % 4, :, :, :].rearrange("d b h s -> d b (h s)")).then_inc(stored[i % 4], 16)

            pairs(body, sp)
            for i in range(4):
                sp.wait_ge(stored[i], 16 * (PAIRS - 1) * PAIR // 4)
            for i in range(2):
                sp.wait_ge(v_stored[i], 16 * PAIR // 2)

        @block.scalar
        def _(act):
            for t in range(PAIR):
                if t == TT:
                    act.wait_ge(angles3, 1)
                    nc.scalar.activation(ang[:, :, :, :], ang[:, :, :, :], ACT.Sin).then_inc(sines3, 1)
                act.wait_ge(tile_done, t + 1)
                if t >= 2:
                    act.wait_ge(v_stored[t % 2], 16 * (t // 2))
                nc.scalar.activation(v_out[:, t % 2, :], p_tile[:, t % 4, :], ACT.Copy).then_inc(tile_taken, 1)

            def normalise(m, i):
                u = (m - 1) * PAIR + i
                act.wait_ge(inv_ready, u + 1)
                for h in range(4):
                    ins = nc.scalar.activation(normed[:, i % 4, h, :], p_tile[:, i % 4, h * D:(h + 1) * D], ACT.Copy,
                                               scale=inv_rms[:, i % 4, h:h + 1])
                ins.then_inc(tile_taken, 1)

            def body(m, first, last):
                for i in range(PAIR):
                    act.wait_ge(tile_done, m * PAIR + i + 1)
                    if not (first and i < 4):
                        act.wait_ge(rotated, (m - 1) * PAIR + i - 3)
                    for h in range(4):
                        ins = nc.scalar.activation(normed[:, i % 4, h, :], p_tile[:, i % 4, h * D:(h + 1) * D], ACT.Square,
                                                   accum_out=squares[:, i % 4, h:h + 1])
                    ins.then_inc(squares_ready, 1)
                    act.wait_ge(squares_ready, (m - 1) * PAIR + i + 1)
                    nc.scalar.activation(rms[:, i % 4, :], squares[:, i % 4, :], ACT.Sqrt, bias=eps[:, :], scale=1.0 / D).then_inc(rms_ready, 1)
                    if i >= 1:
                        normalise(m, i - 1)
                    elif not first:
                        normalise(m - 1, PAIR - 1)

            pairs(body, act)
            normalise(PAIRS - 1, PAIR - 1)

        @block.gpsimd
        def _(pool):
            def split_lo(n, slot, c):
                pool.wait_ge(hi_piece, (n - 1) * EC + c + 1)
                nc.gpsimd.tensor_tensor(w_lo[:, slot, c, :], w_raw[:, slot, c, :], w_hi[:, slot, c, :].bitcast(F32),
                                        ALU.subtract).then_inc(lo_piece, 1)

            for n in range(1, 3):
                for c in range(EC):
                    split_lo(n, n % 2, c)

            def with_sine(m, i, key):
                u = (m - 1) * PAIR + i
                pool.wait_ge(tile_taken, m * PAIR + i + 1)
                if not (isinstance(u, int) and u < 4):
                    pool.wait_ge(rotated, u - 3)
                nc.gpsimd.tensor_tensor(part_b[:, i % 4, :, :], normed[:, i % 4, :, :],
                                        bc(rot[:, key, 1, i % TT, :], 1, [P, 4, D]), ALU.mult).then_inc(b_ready, 1)

            def tiles(m, key, carried, last=False):
                for i in range(PAIR):
                    if i >= 1:
                        with_sine(m, i - 1, key)
                    elif carried:
                        with_sine(m - 1, PAIR - 1, 0)
                    if i % TT < EC and not (last and i >= TT):
                        split_lo(2 * m + 1 + i // TT, (1 + i // TT) % 2, i % TT)

            tiles(1, 1, False)
            with_sine(1, PAIR - 1, 1)
            tiles(2, 0, False)
            _loop(pool, 3, PAIRS - 1, lambda m: tiles(m, 0, True))
            tiles(PAIRS - 1, 0, True, True)
            with_sine(PAIRS - 1, PAIR - 1, 0)

        @block.vector
        def _(v):
            step = Chain(v, step_s)
            def split_hi(n, slot, c):
                if c == 0:
                    if not (isinstance(n, int) and n == 1):
                        v.wait_ge(w_in[slot], 8 * (n - slot))
                        v.wait_ge(tile_done, (n - 1) * TT)
                v.tensor_copy(w_hi[:, slot, c, :], w_raw[:, slot, c, :]).then_inc(hi_piece, 1)

            for c in range(EC):
                split_hi(1, 1, c)
            v.wait_ge(len_in, 16 * 6)
            step(v.tensor_copy(pos[:, :], len_i[:, :]))
            step(v.tensor_scalar(pos[:, :], pos[:, :], cst[:, C_SPOS:C_SPOS + 1], None, ALU.add))
            step(v.memset(eps[:, :], EPS))
            step(v.memset(quarter[:, 0:1], 0.25))
            step(v.memset(quarter[:, 1:2], 0.0))
            for f in range(2):
                step(v.tensor_tensor(ang[:, f, :, :], bc(pos[:, :], 2, [P, TT, D // 2]),
                                     bc(cst[:, C_INVF:C_INVF + D // 2], 1, [P, TT, D // 2]), ALU.mult))
            flat = lambda a: a[:, :, :, :].rearrange("p f t d -> p f (t d)")
            reduce_angle(step, v, flat(ang), flat(turns), bc(quarter[:, :], 2, [P, 2, TT * D // 2]))
            v.engine_nop().then_inc(angles3, 1)
            step(v.tensor_scalar(norm_w[:, 0, :], norm_w[:, 0, :], -SCALE, None, ALU.mult))
            v.wait_ge(sines3, 1)
            for which in range(2):
                for f in range(2):
                    for hf in range(2):
                        at = slice(hf * D // 2, (hf + 1) * D // 2)
                        w = bc(norm_w[:, which, at], 1, [P, TT, D // 2])
                        step(v.tensor_tensor(rot[:, which, f, :, at], ang[:, f, :, :], w, ALU.mult))
                step(v.tensor_scalar(rot[:, which, 1, :, D // 2:D], rot[:, which, 1, :, D // 2:D], -1.0, None, ALU.mult))

            def invert(m, i):
                u = (m - 1) * PAIR + i
                v.wait_ge(rms_ready, u + 1)
                v.reciprocal(inv_rms[:, i % 4, :], rms[:, i % 4, :]).then_inc(inv_ready, 1)

            def rotate(m, i, key):
                u = (m - 1) * PAIR + i
                v.wait_ge(tile_taken, m * PAIR + i + 1)
                if not (isinstance(u, int) and u < 4):
                    v.wait_ge(turned, u - 3)
                v.tensor_tensor(part_a[:, i % 4, :, :], normed[:, i % 4, :, :],
                                bc(rot[:, key, 0, i % TT, :], 1, [P, 4, D]), ALU.mult).then_inc(a_ready, 1)
                v.wait_ge(a_ready, u + 1)
                v.wait_ge(b_ready, u + 1)
                lo, hi = slice(0, D // 2), slice(D // 2, D)
                v.tensor_tensor(part_a[:, i % 4, :, lo], part_a[:, i % 4, :, lo], part_b[:, i % 4, :, hi], ALU.add).then_inc(half_rotated, 1)
                v.tensor_tensor(part_a[:, i % 4, :, hi], part_a[:, i % 4, :, hi], part_b[:, i % 4, :, lo], ALU.add).then_inc(rotated, 1)

            def put(m, i):
                u = (m - 1) * PAIR + i
                v.wait_ge(turned, u + 1)
                if not (isinstance(u, int) and u < 4):
                    v.wait_ge(stored[i % 4], 4 * (u - i % 4))
                v.tensor_copy(stage[:, i % 4, :, :, :].rearrange("p b h s -> p h b s"),
                              p_turn[:, i % 2, :, :].rearrange("p h (b s) -> p h b s", s=S)).then_inc(staged, 1)

            def at(m, i, first, act_on, *more):
                if i >= 0:
                    act_on(m, i, *more)
                elif not first:
                    act_on(m - 1, PAIR + i, *more)

            def tiles(m, key, rotates_before, puts_before, last=False):
                for i in range(PAIR):
                    at(m, i - 4, not puts_before, put)
                    if i % TT < EC and not (last and i >= TT):
                        split_hi(2 * m + 1 + i // TT, (1 + i // TT) % 2, i % TT)
                    invert(m, i)
                    at(m, i - 2, not rotates_before, rotate, key)

            for c in range(EC):
                split_hi(2, 0, c)
            tiles(1, 1, False, False)
            for i in range(PAIR - 2, PAIR):
                rotate(1, i, 1)
            tiles(2, 0, False, True)
            _loop(v, 3, PAIRS - 1, lambda m: tiles(m, 0, True, True))
            tiles(PAIRS - 1, 0, True, True, True)
            for i in range(PAIR, PAIR + 4):
                put(PAIRS - 1, i - 4)
                if i < PAIR + 2:
                    rotate(PAIRS - 1, i - 2, 0)

        @block.tensor
        def _(pe):
            def project(m, i):
                t = m * PAIR + i
                if i % TT == 0 and not (isinstance(t, int) and t == 0):
                    pe.wait_ge(lo_piece, (2 * m + i // TT) * EC)
                if not (isinstance(t, int) and t < 4):
                    pe.wait_ge(tile_taken, t - 3)
                rows = slice(i % TT * P, (i % TT + 1) * P)
                for c in range(EC):
                    mm = three_pass(pe, p_tile[:, i % 4, :], x_hi[:, c, rows], x_lo[:, c, rows],
                                    w_hi[:, i // TT, c, :], w_lo[:, i // TT, c, :], c == 0, c == EC - 1)
                mm.then_inc(tile_done, 1)

            def turn(m, i):
                u = (m - 1) * PAIR + i
                pe.wait_ge(rotated, u + 1)
                if not (isinstance(u, int) and u < 2):
                    pe.wait_ge(staged, u - 1)
                for h in range(4):
                    mm = pe.transpose(p_turn[:, i % 2, h, :], part_a[:, i % 4, h, :], ident)
                mm.then_inc(turned, 1)

            for i in range(PAIR):
                project(0, i)

            def body(m, first, last):
                for i in range(PAIR):
                    project(m, i)
                    if i >= LAG:
                        turn(m, i - LAG)
                    elif not first:
                        turn(m - 1, PAIR + i - LAG)

            body(1, True, False)
            _loop(pe, 2, PAIRS, lambda m: body(m, False, False))
            for i in range(PAIR - LAG, PAIR):
                turn(PAIRS - 1, i)


class OutputWeights:

    def __init__(self, ctx, nc):
        self.raw = ctx.enter_context(nc.sbuf_tensor("wo_raw", [P, 2, G, E], F32))
        self.hi = ctx.enter_context(nc.sbuf_tensor("wo_hi", [P, 2, G, E], F32R))
        self.lo = ctx.enter_context(nc.sbuf_tensor("wo_lo", [P, 2, G, E], F32R))
        self.head_0 = ctx.enter_context(nc.sbuf_tensor("o_head_0", [P, B, G * S], F32))


def cached_attention(nc, io, cst, wo):
    with ExitStack() as ctx:
        sb = lambda name, shape, dt=F32: ctx.enter_context(nc.sbuf_tensor(name, shape, dt))
        sem = lambda name: ctx.enter_context(nc.semaphore(name))
        KW = HK * S
        keys = sb("keys", [P, 2, NPP + 1, HK, S])
        vals = sb("vals", [P, 2, NPP // 4 + 1, HK * D])
        queries = sb("queries", [P, 2, HQ * S])
        outs = sb("outs", [P, 2, HQ * S])
        pages = sb("pages", [P, B * NPP], I32)
        pages_f = sb("pages_f", [P, B * NPP])
        rows = sb("rows", [P, B, NPP // 4 + NPP], I32)
        rows_now = sb("rows_now", [P, 2, NPP // 4 + NPP], I32)
        len_i = sb("len4_i", [P, B], I32)
        len_f = sb("len4_f", [P, B])
        mask = sb("mask", [P, 2, KEYS])
        probs = sb("probs4", [P, 2, KEYS])
        low = sb("low", [P, 2])
        wait_carrier = sb("wait_carrier", [P, 1])
        pool_carrier = sb("pool_carrier", [P, 4])
        total = sb("total4", [P, 2])
        inverse = sb("inverse4", [P, 2])
        probs_t = sb("probs4_t", [P, 2, 5, P])
        p_score = ctx.enter_context(nc.psum_tensor("p4_score", [P, 2, 2 * E], F32))
        p_turn = ctx.enter_context(nc.psum_tensor("p4_turn", [P, 2, 4, P], F32))
        p_val = ctx.enter_context(nc.psum_tensor("p4_val", [P, 2, E], F32))
        ident = cst[:, C_ID:C_ID + P]

        table_in = sem("table_in")
        kq_in = [sem(f"kq_in{i}") for i in range(2)]
        v_new_in = [sem(f"v_new_in{i}") for i in range(2)]
        keys_gathered = [sem(f"keys_gathered{i}") for i in range(2)]
        vals_gathered = [sem(f"vals_gathered{i}") for i in range(2)]
        len_ready = sem("len_ready")
        pages_ready = sem("pages_ready")
        rows_ready = sem("rows_ready")
        rows_placed = sem("rows_placed")
        mask_ready = sem("mask_ready")
        scores_done = sem("scores4_done")
        masked = sem("masked4")
        exp_done = sem("exp4_done")
        inverse_ready = sem("inverse4_ready")
        probs_ready = sem("probs4_ready")
        turned = sem("turned4")
        main_taken = sem("main_taken")
        new_taken = sem("new_taken")
        val_done = sem("val4_done")
        out_ready = sem("out4_ready")
        out_stored = [sem(f"out_stored{i}") for i in range(2)]
        wo_in = sem("wo_in")
        wo_hi_ready = sem("wo_hi_ready")
        wo_lo_ready = sem("wo_lo_ready")

        SP_PAGES = range(0, NPP, 2)
        LOADS = 16 * (len(SP_PAGES) + 2)
        GATHERS = 16 * (NPP - len(SP_PAGES))
        VALS = 16 * (NPP // 4)
        RB = 2 * HK
        k_pages, v_pages = io["k_pages"], io["v_pages"]
        qk, v_new, o_dram = io["qk_new"], io["v_new"], io["o_new"]
        both = lambda body, eng: (body(0, True), _loop(eng, 1, B // 2, lambda m: body(m, False)))

        block = ctx.enter_context(nc.Block())

        @block.sync
        def _(sp):
            sp.dma_start(pages[:, :], io["block_table"].partition_broadcast(P)).then_inc(table_in, 16)
            sp.dma_start(len_i[:, :], io["cache_len"].partition_broadcast(P)).then_inc(table_in, 16)
            sp.wait_ge(table_in, 32)

            def store(m, slot):
                sp.wait_ge(out_ready, m * RB + (slot + 1) * HK)
                b = sp.snap(2 * m + slot) if not isinstance(m, int) else 2 * m + slot
                sp.dma_start(o_dram[bass.ds(b, 1), :, :].rearrange("o d n -> (o d) n"), outs[:, slot, :]).then_inc(out_stored[slot], 16)
                sp.dma_start(wo.head_0[:, bass.ds(b, 1), :].rearrange("p o n -> p (o n)"), outs[:, slot, 0:G * S]).then_inc(out_stored[slot], 16)

            def body(m, first):
                for slot in range(2):
                    b = 2 * m + slot
                    done = kq_in[slot]
                    if not first:
                        sp.wait_ge(scores_done, (b - 1) * HK)
                    mine = qk[bass.ds(b, 1), :, :].rearrange("o d n -> (o d) n")
                    sp.dma_start(queries[:, slot, :], mine[:, KW:KW + HQ * S]).then_inc(done, 16)
                    sp.dma_start(keys[:, slot, NPP, :, :].rearrange("p h s -> p (h s)"), mine[:, 0:KW]).then_inc(done, 16)
                    for j in SP_PAGES:
                        page = sp.value_load(pages[0:1, bass.ds(b * NPP + j, 1)], min_val=0, max_val=PAGES - 1)
                        sp.dma_start(keys[:, slot, j, :, :].rearrange("p h s -> p (h s)"),
                                     k_pages[bass.ds(page, 1), :, :].rearrange("o d n -> (o d) n")).then_inc(done, 16)
                    row = sp.snap(b * S)
                    if not first:
                        store(m - 1, slot)
                    sp.dma_start(vals[0:S, slot, NPP // 4, :], v_new[bass.ds(row, S), :]).then_inc(v_new_in[slot], 16)

            body(0, True)
            sp.dma_start(wo.raw[:, :, :, :], io["w_o_t"][0:2 * G * P, :].rearrange("(s g p) n -> p s g n", s=2, p=P)).then_inc(wo_in, 16)
            _loop(sp, 1, B // 2, lambda m: body(m, False))
            for slot in range(2):
                store(B // 2 - 1, slot)
            for slot in range(2):
                sp.wait_ge(out_stored[slot], 32 * B // 2)

        @block.gpsimd
        def _(pool):
            k_flat = k_pages.rearrange("o d n -> (o d) n")
            v_flat = v_pages.rearrange("o t n -> (o t) n")

            def gather(to, rows, source, done):
                pool.indirect_dma_start(to, None, source, bass.IndirectOffsetOnAxis(ap=rows, axis=0)).then_inc(done, 16)

            def hold_wait(n):
                one = pool_carrier[:, 2:3]
                nc.gpsimd.tensor_tensor(pool_carrier[:, n:n + 1], one, one, ALU.mult)

            pool.wait_ge(rows_ready, 5)
            pool.wait_ge(len_ready, 1)

            def body(m, first):
                for slot in range(2):
                    b = 2 * m + slot
                    if not first:
                        pool.wait_ge(scores_done, (b - 1) * HK)
                    row = pool.snap(b) if not first else b
                    if not first:
                        hold_wait(0)
                    nc.gpsimd.tensor_copy(rows_now[:, slot, :], rows[:, bass.ds(row, 1), :].rearrange("p o n -> p (o n)")).then_inc(rows_placed, 1)
                    pool.wait_ge(rows_placed, b + 1)
                    hold_wait(1)
                    for j in range(NPP):
                        if j not in SP_PAGES:
                            gather(keys[:, slot, j, :, :].rearrange("p h s -> p (h s)"),
                                   rows_now[:, slot, NPP // 4 + j:NPP // 4 + j + 1], k_flat, keys_gathered[slot])
                    if not first:
                        pool.wait_ge(val_done, (b - 1) * HK)
                        hold_wait(3)
                    for n in range(NPP // 4):
                        gather(vals[:, slot, n, :], rows_now[:, slot, n:n + 1], v_flat, vals_gathered[slot])

            body(0, True)
            _loop(pool, 1, B // 2, lambda m: body(m, False))
            for slot in range(2):
                pool.wait_ge(wo_hi_ready, slot + 1)
                nc.gpsimd.tensor_tensor(wo.lo[:, slot, :, :], wo.raw[:, slot, :, :], wo.hi[:, slot, :, :].bitcast(F32),
                                        ALU.subtract).then_inc(wo_lo_ready, 1)

        def step_of(m, i, first, what):
            if i >= 0:
                what(m, i)
            elif not first:
                what(m - 1, RB + i)

        @block.scalar
        def _(act):
            def exponent(m, i):
                r = m * RB + i
                act.wait_ge(masked, r + 1)
                nc.scalar.activation(probs[:, i % 2, :], probs[:, i % 2, :], ACT.Exp, bias=low[:, i % 2:i % 2 + 1],
                                     scale=-1.0, accum_out=total[:, i % 2:i % 2 + 1]).then_inc(exp_done, 1)

            def take_turned(m, i):
                r = m * RB + i
                act.wait_ge(turned, r + 1)
                if not (isinstance(r, int) and r < 2):
                    act.wait_ge(val_done, r - 1)
                nc.scalar.activation(probs_t[:, i % 2, 0:4, :], p_turn[:, 0, :, :], ACT.Copy).then_inc(main_taken, 1)

            def take_values(m, i):
                r = m * RB + i
                slot, k = i // HK, i % HK
                act.wait_ge(val_done, r + 1)
                if k == 0 and not (isinstance(m, int) and m == 0):
                    act.wait_ge(out_stored[slot], 32 * m)
                nc.scalar.activation(outs[:, slot, k * P:(k + 1) * P], p_val[:, i % 2, 0:P], ACT.Copy).then_inc(out_ready, 1)

            def body(m, first):
                for i in range(RB):
                    exponent(m, i)
                    step_of(m, i - 1, first, take_turned)
                    step_of(m, i - 2, first, take_values)

            body(0, True)
            act.wait_ge(wo_in, 16)
            for slot in range(2):
                nc.scalar.activation(wo.hi[:, slot, :, :], wo.raw[:, slot, :, :], ACT.Copy).then_inc(wo_hi_ready, 1)
            _loop(act, 1, B // 2, lambda m: body(m, False))
            take_turned(B // 2 - 1, RB - 1)
            take_values(B // 2 - 1, RB - 2)
            take_values(B // 2 - 1, RB - 1)


        @block.vector
        def _(v):
            v.memset(pool_carrier[:, :], 1.0).then_inc(len_ready, 1)
            v.wait_ge(table_in, 32)
            v.tensor_copy(len_f[:, :], len_i[:, :]).then_inc(len_ready, 1)
            v.tensor_copy(pages_f[:, :], pages[:, :]).then_inc(pages_ready, 1)
            v.wait_ge(pages_ready, 1)
            v.tensor_scalar(rows[:, :, NPP // 4:], pages_f[:, :].rearrange("p (b j) -> p b j", b=B), float(D), cst[:, C_PART:C_PART + 1], ALU.mult, ALU.add).then_inc(rows_ready, 1)
            for q in range(4):
                at = slice(S * q, S * q + S)
                v.tensor_scalar(rows[at, :, 0:NPP // 4], pages_f[at, :].rearrange("p (b n q) -> p q b n", b=B, q=4)[:, q], float(PSIZE),
                                cst[at, C_SPOS:C_SPOS + 1], ALU.mult, ALU.add).then_inc(rows_ready, 1)
            v.wait_ge(len_ready, 2)

            def make_mask(m, slot):
                b = 2 * m + slot
                v.tensor_scalar(mask[:, slot, :], cst[:, C_KEYPOS:C_KEYPOS + KEYS], len_f[:, bass.ds(b, 1)], BIG,
                                ALU.is_ge, ALU.mult).then_inc(mask_ready, 1)

            def mask_scores(m, i):
                r = m * RB + i
                v.wait_ge(scores_done, r + 1)
                if not (isinstance(r, int) and r < 2):
                    v.wait_ge(turned, r - 1)
                v.memset(wait_carrier[:, :], 0.0)
                v.tensor_tensor_reduce(out=probs[:, i % 2, :], in0=p_score[:, i % 2, 0:KEYS], in1=mask[:, i // HK, :],
                                       scale=1.0, scalar=3e38, op0=ALU.add, op1=ALU.min,
                                       accum_out=low[:, i % 2:i % 2 + 1]).then_inc(masked, 1)

            def normalise(m, i):
                r = m * RB + i
                v.wait_ge(exp_done, r + 1)
                v.reciprocal(inverse[:, i % 2:i % 2 + 1], total[:, i % 2:i % 2 + 1]).then_inc(inverse_ready, 1)
                v.wait_ge(inverse_ready, r + 1)
                v.tensor_scalar(probs[:, i % 2, :], probs[:, i % 2, :], inverse[:, i % 2:i % 2 + 1], None,
                                ALU.mult).then_inc(probs_ready, 1)

            def take_new(m, i):
                r = m * RB + i
                v.wait_ge(turned, r + 1)
                if not (isinstance(r, int) and r < 2):
                    v.wait_ge(val_done, r - 1)
                v.tensor_copy(probs_t[0:S, i % 2, 4, :], p_turn[0:S, 1, 0, :]).then_inc(new_taken, 1)

            def body(m, first):
                for i in range(RB):
                    if i % HK == 0:
                        make_mask(m, i // HK)
                        v.wait_ge(mask_ready, 2 * m + i // HK + 1)
                    mask_scores(m, i)
                    step_of(m, i - 1, first, take_new)
                    normalise(m, i)

            both(body, v)
            take_new(B // 2 - 1, RB - 1)

        @block.tensor
        def _(pe):
            def scores(m, i):
                r = m * RB + i
                slot, k = i // HK, i % HK
                if k == 0:
                    pe.wait_ge(kq_in[slot], LOADS * m + LOADS)
                    pe.wait_ge(keys_gathered[slot], GATHERS * m + GATHERS)
                if not (isinstance(r, int) and r < 2):
                    pe.wait_ge(masked, r - 1)
                q = queries[:, slot, k * P:(k + 1) * P]
                pe.matmul(p_score[:, i % 2, 0:CACHE], q, keys[:, slot, 0:NPP, k, :], start=True, stop=True)
                pe.matmul(p_score[:, i % 2, CACHE:KEYS], q, keys[:, slot, NPP, k, :], start=True, stop=True).then_inc(scores_done, 1)

            def transposes(m, i):
                r = m * RB + i
                pe.wait_ge(probs_ready, r + 1)
                if not (isinstance(r, int) and r < 1):
                    pe.wait_ge(main_taken, r)
                    pe.wait_ge(new_taken, r)
                for n in range(4):
                    pe.transpose(p_turn[:, 0, n, :], probs[:, i % 2, n * P:(n + 1) * P], ident)
                pe.transpose(p_turn[0:S, 1, 0, :], probs[:, i % 2, CACHE:KEYS], ident).then_inc(turned, 1)

            def values(m, i):
                r = m * RB + i
                slot, k = i // HK, i % HK
                if k == 0:
                    pe.wait_ge(vals_gathered[slot], VALS * m + VALS)
                    pe.wait_ge(v_new_in[slot], 16 * m + 16)
                pe.wait_ge(main_taken, r + 1)
                pe.wait_ge(new_taken, r + 1)
                if not (isinstance(r, int) and r < 2):
                    pe.wait_ge(out_ready, r - 1)
                cols = slice(k * D, (k + 1) * D)
                for n in range(4):
                    pe.matmul(p_val[:, i % 2, 0:P], vals[:, slot, n, cols], probs_t[:, i % 2, n, :], start=(n == 0), stop=False)
                pe.matmul(p_val[:, i % 2, 0:P], vals[0:S, slot, 4, cols], probs_t[0:S, i % 2, 4, :], start=False,
                          stop=True).then_inc(val_done, 1)

            def body(m, first):
                for i in range(RB):
                    scores(m, i)
                    step_of(m, i - 1, first, transposes)
                    step_of(m, i - 2, first, values)

            both(body, pe)
            transposes(B // 2 - 1, RB - 1)
            values(B // 2 - 1, RB - 2)
            values(B // 2 - 1, RB - 1)


def output_ffn(nc, io, x_res, wo):
    with ExitStack() as ctx:
        sb = lambda name, shape, dt=F32: ctx.enter_context(nc.sbuf_tensor(name, shape, dt))
        sem = lambda name: ctx.enter_context(nc.semaphore(name))
        o_odd = sb("o_odd", [P, B, G * S])
        o_raw = (wo.head_0, o_odd)
        o_hi = sb("o5_hi", [P, B, G * S], F32R)
        o_lo = sb("o5_lo", [P, B, G * S], F32R)
        w_raw, w_hi, w_lo = wo.raw, wo.hi, wo.lo
        y3 = sb("y3", [P, EC, TOK])
        lora_a = sb("lora_a", [P, E])
        lora_b = sb("lora_b", [P, E])
        lora_c = sb("lora_c", [P, 1])
        w_ffn = sb("w_ffn", [P, EC, E])
        bias = sb("bias", [P, EC])
        p_out = ctx.enter_context(nc.psum_tensor("p_out", [P, 4, E], F32))
        p_lora = ctx.enter_context(nc.psum_tensor("p_lora", [P, 4, E], F32))

        o_in = [sem(f"o5_in{i}") for i in range(2)]
        w_in = [sem(f"w5_in{i}") for i in range(2)]
        ffn_in = sem("ffn_in")
        o_hi_ready = sem("o5_hi_ready")
        o_lo_ready = sem("o5_lo_ready")
        w_hi_ready = sem("w5_hi_ready")
        w_lo_ready = sem("w5_lo_ready")
        out_done = sem("out5_done")
        out_added = sem("out5_added")
        lora_step = sem("lora_step")
        lora_done = sem("lora_done")
        ffn_ready = sem("ffn_ready")
        ffn_done = sem("ffn_done")
        final_ready = sem("final_ready")
        final_out = sem("final_out")
        OT = 2 * EC
        PAIRS = HK // 2
        w_o = io["w_o_t"].rearrange("(m p) n -> p m n", p=P)
        o_all = io["o_new"].rearrange("b d n -> d b n")
        halves = [slice(0, B // 2), slice(B // 2, B)]
        tokens = [slice(0, HALF), slice(HALF, TOK)]
        heads = lambda body, eng: (body(0, True, False), _loop(eng, 1, PAIRS - 1, lambda m: body(m, False, False)),
                                   body(PAIRS - 1, False, True))

        block = ctx.enter_context(nc.Block())

        @block.sync
        def _(sp):
            sp.dma_start(o_odd[:, :, :], o_all[:, :, P:2 * P]).then_inc(o_in[1], 16)
            for to, name in ((lora_a[:, :], "lora_a"), (lora_b[:, :], "lora_b_t")):
                sp.dma_start(to, io[name]).then_inc(ffn_in, 16)
            lw = io["lora_w"]
            sp.dma_start(lora_c[:, :], bc(lw, 1, [LORA_N, RANK]).unsqueeze(2), allow_slow_non_contiguous=True).then_inc(ffn_in, 16)
            sp.dma_start(w_ffn[:, :, :], io["w_ffn_t"].rearrange("(c p) n -> p c n", p=P)).then_inc(ffn_in, 16)
            sp.dma_start(bias[:, :], io["bias"].rearrange("(c p) -> p c", p=P), allow_slow_non_contiguous=True).then_inc(ffn_in, 16)

            def body(m, first, last):
                for slot in range(2):
                    k = 2 * m + slot
                    oc, wr = sp.snap(k * P + 2 * P), sp.snap(k * G + 2 * G)
                    if not first:
                        sp.wait_ge(w_lo_ready, k - 1)
                    sp.dma_start(w_raw[:, slot, :, :], w_o[:, bass.ds(wr, G), :]).then_inc(w_in[slot], 16)
                    sp.wait_ge(o_lo_ready, 2 * k + 2)
                    sp.dma_start(o_raw[slot][:, :, :], o_all[:, :, bass.ds(oc, P)]).then_inc(o_in[slot], 16)

            body(0, True, False)
            _loop(sp, 1, PAIRS - 1, lambda m: body(m, False, False))
            rows = io["out_t"].rearrange("(c p) n -> p c n", p=P)
            for i in range(OT):
                sp.wait_ge(final_ready, i + 1)
                sp.dma_start(rows[:, i % EC, tokens[i // EC]], x_res[:, i % EC, tokens[i // EC]]).then_inc(final_out, 16)
            sp.wait_ge(final_out, 16 * OT)

        @block.scalar
        def _(act):
            def body(m, first, last):
                for slot in range(2):
                    k = 2 * m + slot
                    start = first and slot == 0
                    if not first:
                        act.wait_ge(w_in[slot], 16 * m)
                        act.wait_ge(out_done, OT * (k - 1))
                        nc.scalar.activation(w_hi[:, slot, :, :], w_raw[:, slot, :, :], ACT.Copy).then_inc(w_hi_ready, 1)
                    if not start:
                        act.wait_ge(o_in[slot], 16 * (m + slot))
                    for hf in range(2):
                        if not start:
                            act.wait_ge(out_done, OT * (k - 1) + EC * (hf + 1))
                        nc.scalar.activation(o_hi[:, halves[hf], :], o_raw[slot][:, halves[hf], :], ACT.Copy).then_inc(o_hi_ready, 1)

            heads(body, act)

        @block.gpsimd
        def _(pool):
            def body(m):
                for slot in range(2):
                    pool.wait_ge(w_hi_ready, 2 * m + slot - 1)
                    nc.gpsimd.tensor_tensor(w_lo[:, slot, :, :], w_raw[:, slot, :, :], w_hi[:, slot, :, :].bitcast(F32),
                                            ALU.subtract).then_inc(w_lo_ready, 1)

            _loop(pool, 1, PAIRS, body)

        @block.vector
        def _(v):
            def split_o(k, slot, hf):
                v.wait_ge(o_hi_ready, 2 * k + hf + 1)
                v.tensor_tensor(o_lo[:, halves[hf], :], o_raw[slot][:, halves[hf], :], o_hi[:, halves[hf], :].bitcast(F32),
                                ALU.subtract).then_inc(o_lo_ready, 1)

            def body(m, first, last):
                for slot in range(2):
                    k = 2 * m + slot
                    for i in range(OT):
                        v.wait_ge(out_done, OT * k + i + 1)
                        at = y3[:, i % EC, tokens[i // EC]]
                        if first and slot == 0:
                            v.tensor_copy(at, p_out[:, i % 4, :]).then_inc(out_added, 1)
                        else:
                            v.tensor_tensor(at, at, p_out[:, i % 4, :], ALU.add).then_inc(out_added, 1)
                        if i % EC == EC - 1 and not (last and slot == 1):
                            split_o(k + 1, 1 - slot, i // EC)

            for hf in range(2):
                split_o(0, 0, hf)
            v.wait_ge(ffn_in, 16 * 5)
            v.tensor_scalar(lora_c[:, :], lora_c[:, :], LORA_SCALE, None, ALU.mult).then_inc(lora_step, 1)
            v.wait_ge(lora_step, 1)
            v.tensor_scalar(lora_b[:, :], lora_b[:, :], lora_c[:, 0:1], None, ALU.mult).then_inc(lora_step, 1)
            body(0, True, False)
            v.wait_ge(lora_done, 1)
            v.tensor_tensor(w_ffn[:, :, :], w_ffn[:, :, :], p_lora[:, :, :], ALU.add).then_inc(ffn_ready, 1)
            _loop(v, 1, PAIRS - 1, lambda m: body(m, False, False))
            body(PAIRS - 1, False, True)
            for i in range(OT):
                v.wait_ge(ffn_done, i + 1)
                at = x_res[:, i % EC, tokens[i // EC]]
                v.scalar_tensor_tensor(out=at, in0=p_out[:, i % 4, :], scalar=bias[:, i % EC:i % EC + 1], in1=at,
                                       op0=ALU.add, op1=ALU.add).then_inc(final_ready, 1)

        @block.tensor
        def _(pe):
            def body(m, first, last):
                for slot in range(2):
                    k = 2 * m + slot
                    if not first:
                        pe.wait_ge(w_lo_ready, k - 1)
                    for i in range(OT):
                        if i % EC == 0:
                            pe.wait_ge(o_lo_ready, 2 * k + i // EC + 1)
                        if not (first and slot == 0 and i < 4):
                            pe.wait_ge(out_added, k * OT + i - 3)
                        to = slice(i % EC * P, (i % EC + 1) * P)
                        bs = halves[i // EC]
                        for g in range(G):
                            gs = slice(g * S, (g + 1) * S)
                            mm = three_pass(pe, p_out[:, i % 4, :], w_hi[:, slot, g, to], w_lo[:, slot, g, to],
                                            o_hi[:, bs, gs], o_lo[:, bs, gs], g == 0, g == G - 1)
                        mm.then_inc(out_done, 1)

            body(0, True, False)
            pe.wait_ge(lora_step, 2)
            for c in range(EC):
                mm = pe.matmul(p_lora[:, c, :], lora_a[:, c * P:(c + 1) * P], lora_b[:, :], start=True, stop=True)
            mm.then_inc(lora_done, 1)
            _loop(pe, 1, PAIRS, lambda m: body(m, False, False))
            pe.wait_ge(ffn_ready, 1)
            for i in range(OT):
                pe.wait_ge(out_added, HK * OT - 3 + i if i < 4 else HK * OT)
                if i >= 4:
                    pe.wait_ge(final_ready, i - 3)
                for c in range(EC):
                    mm = pe.matmul(p_out[:, i % 4, :], w_ffn[:, c, i % EC * P:(i % EC + 1) * P],
                                   y3[:, c, tokens[i // EC]], start=(c == 0), stop=(c == EC - 1))
                mm.then_inc(ffn_done, 1)


def layouts(inputs):
    def lay(a):
        return np.ascontiguousarray(a)

    x = np.asarray(inputs["x"])
    u = x.transpose(2, 1, 0).reshape(EC, P, S * B)[:, ::-1]
    wqkv = np.asarray(inputs["L0_attn_w_qkv"]).T
    c = np.asarray(inputs["L0_cond_C"])
    return {
        "xT": lay(x.reshape(TOK, E).T),
        "u_rev": lay(u.reshape(E, S * B)),
        "length": lay(inputs["itok_B_78_3631"]),
        "log_dt_b": lay(inputs["L0_cond_log_dt"]),
        "log_A_real_t": lay(np.asarray(inputs["L0_cond_log_A_real"]).T),
        "A_imag_t": lay(np.asarray(inputs["L0_cond_A_imag"]).T),
        "C_re_t": lay(c[..., 0].T),
        "C_im_t": lay(c[..., 1].T),
        "D": lay(inputs["L0_cond_D"]),
        "w_qkv_t": lay(wqkv),
        "w_dense_t": lay(np.asarray(inputs["L0_attn_w_dense"]).T),
        "w_vkq_t": lay(np.concatenate([inputs["L0_cond2_Wv"], inputs["L0_cond2_Wk"], inputs["L0_cond2_Wq"]]).T),
        "cache_len": lay(inputs["itok_B_207_1644"]),
        "block_table": lay(np.asarray(inputs["itok_Bx16_0_63"]).reshape(B * NPP)),
        "q_norm": lay(inputs["L0_cond2_q_norm_w"]),
        "k_norm": lay(inputs["L0_cond2_k_norm_w"]),
        "k_pages": lay(np.asarray(inputs["L0_cond2_k_cache"]).transpose(0, 3, 2, 1).reshape(PAGES, D, HK * PSIZE)),
        "v_pages": lay(np.asarray(inputs["L0_cond2_v_cache"]).reshape(PAGES, PSIZE, HK * D)),
        "w_o_t": lay(np.asarray(inputs["L0_cond2_Wo"]).T),
        "lora_a": lay(np.asarray(inputs["L0_ffn_lora_A"]).reshape(LORA_N * RANK, E)),
        "lora_b_t": lay(np.asarray(inputs["L0_ffn_lora_B"]).transpose(0, 2, 1).reshape(LORA_N * RANK, E)),
        "lora_w": lay(inputs["L0_ffn_lora_weights"]),
        "w_ffn_t": lay(np.asarray(inputs["L0_ffn_W"]).T),
        "bias": lay(inputs["L0_ffn_bias"]),
        "cst": constants(),
    }


def build(nc, io):
    io["kpad"] = nc.dram_tensor("kpad", (S * (P + E),), F32, kind="Internal").ap()
    io["v_attn"] = nc.dram_tensor("v_attn", (TOK, HK * D), F32, kind="Internal").ap()
    io["v_new"] = nc.dram_tensor("v_new", (TOK, HK * D), F32, kind="Internal").ap()
    io["qk_new"] = nc.dram_tensor("qk_new", (B, D, (HK + HQ) * S), F32, kind="Internal").ap()
    io["o_new"] = nc.dram_tensor("o_new", (B, D, HQ * S), F32, kind="Internal").ap()
    with ExitStack() as ctx:
        cst = ctx.enter_context(nc.sbuf_tensor("cst", [P, C_COLS], F32))
        x_res = ctx.enter_context(nc.sbuf_tensor("x_res", [P, EC, TOK], F32))
        with ExitStack() as ctx2:
            y_hi = ctx2.enter_context(nc.sbuf_tensor("y_hi", [P, EC, TOK], F32R))
            y_lo = ctx2.enter_context(nc.sbuf_tensor("y_lo", [P, EC, TOK], F32R))
            weights = Weights(ctx2, nc)
            ssm_conv(nc, io, cst, x_res, y_hi, y_lo, weights)
            gqa(nc, io, cst, x_res, y_hi, y_lo, weights)
            cached_qkv(nc, io, cst, y_hi, y_lo, weights)
        wo = OutputWeights(ctx, nc)
        cached_attention(nc, io, cst, wo)
        output_ffn(nc, io, x_res, wo)


def kernel(**inputs):
    import concourse.bacc as bacc
    from concourse.bass_utils import run_bass_kernel_spmd

    nc = bacc.Bacc("TRN2", target_bir_lowering=False, num_devices=1)
    arrays, io = {}, {}
    for name, a in layouts(inputs).items():
        arrays[f"in_{name}"] = a
        io[name] = nc.dram_tensor(f"in_{name}", a.shape, mybir.dt.from_np(a.dtype), kind="ExternalInput").ap()
    io["out_t"] = nc.dram_tensor("out_t", (E, TOK), F32, kind="ExternalOutput").ap()
    build(nc, io)
    r = run_bass_kernel_spmd(nc, [arrays], core_ids=[0])
    return np.ascontiguousarray(r.results[0]["out_t"].T).reshape(B, S, E)
```
